# Optimizing a Trainium2 kernel written in Bass

```python
import numpy as np
import jax
import jax.numpy as jnp

def _softmax(x, axis=-1):
    return jax.nn.softmax(x, axis=axis)

def _gelu(x):
    return jax.nn.gelu(x, approximate=True)

def _silu(x):
    return jax.nn.silu(x)

def _sigmoid(x):
    return jax.nn.sigmoid(x)

def _layernorm(x, axis=-1, eps=1e-05):
    m = jnp.mean(x, axis=axis, keepdims=True)
    v = jnp.var(x, axis=axis, keepdims=True)
    return (x - m) / jnp.sqrt(v + eps)

def _scatter_add(tgt, idx, src, axis=0):
    return tgt.at[idx].add(src)

def _segment_sum(src, seg, n):
    return jax.ops.segment_sum(src, seg, n)
kernel_name = 'mk_seq_preln_d1_jaxref_r8_f338ad'

def setup_inputs(seed: int=0):
    np.random.seed(seed)
    _w = jnp.asarray

    def _L0_attn_setup():
        import jax, jax.numpy as jnp
        import numpy as np
        B, S, E, H, D = (4, 256, 128, 16, 64)

        def _large_negative_number(dtype):
            return jnp.asarray(-0.7 * jnp.finfo(dtype).max, dtype=dtype)
        key = jax.random.key(seed)
        k1, k2, k3 = jax.random.split(key, 3)
        x = jax.random.normal(k1, (B, S, E), dtype=jnp.float32)
        qkv_w = jax.random.normal(k2, (E, H, 3 * D), dtype=jnp.float32) * (1.0 / np.sqrt(E))
        qkv_b = jnp.zeros((H, 3 * D), dtype=jnp.float32)
        out_w = jax.random.normal(k3, (H, D, E), dtype=jnp.float32) * (1.0 / np.sqrt(H * D))
        out_b = jnp.zeros((E,), dtype=jnp.float32)
        return {'x': x, 'qkv_w': qkv_w, 'qkv_b': qkv_b, 'out_w': out_w, 'out_b': out_b}
    _L0_attn_in = _L0_attn_setup()

    def _L0_ffn_setup():
        import jax, jax.numpy as jnp
        import numpy as np
        TOP_K = 2

        def _ffn(x, gw, uw, dw):
            return jax.nn.silu(x @ gw.T) * (x @ uw.T) @ dw.T
        key = jax.random.key(seed)
        ks = jax.random.split(key, 8)
        w = lambda k, shape: jax.random.normal(k, shape, jnp.float32) * 0.02
        return dict(x=jax.random.normal(ks[0], (4, 256, 128), jnp.float32), gate_w=w(ks[1], (8, 128)), expert_gate=w(ks[2], (8, 352, 128)), expert_up=w(ks[3], (8, 352, 128)), expert_down=w(ks[4], (8, 128, 352)), shared_gate=w(ks[5], (352, 128)), shared_up=w(ks[6], (352, 128)), shared_down=w(ks[7], (128, 352)))
    _L0_ffn_in = _L0_ffn_setup()
    _d = {'L0_attn_x': _L0_attn_in['x'], 'L0_attn_qkv_w': _L0_attn_in['qkv_w'], 'L0_attn_qkv_b': _L0_attn_in['qkv_b'], 'L0_attn_out_w': _L0_attn_in['out_w'], 'L0_attn_out_b': _L0_attn_in['out_b'], 'L0_ffn_gate_w': _L0_ffn_in['gate_w'], 'L0_ffn_expert_gate': _L0_ffn_in['expert_gate'], 'L0_ffn_expert_up': _L0_ffn_in['expert_up'], 'L0_ffn_expert_down': _L0_ffn_in['expert_down'], 'L0_ffn_shared_gate': _L0_ffn_in['shared_gate'], 'L0_ffn_shared_up': _L0_ffn_in['shared_up'], 'L0_ffn_shared_down': _L0_ffn_in['shared_down']}
    _x0 = _d['L0_attn_x']
    _d['L0_attn_x'] = jax.random.normal(jax.random.fold_in(jax.random.key(seed), 1), (1, 2048, 128), dtype=_x0.dtype)
    del _x0
    return _d

def reference(L0_attn_x, L0_attn_qkv_w, L0_attn_qkv_b, L0_attn_out_w, L0_attn_out_b, L0_ffn_gate_w, L0_ffn_expert_gate, L0_ffn_expert_up, L0_ffn_expert_down, L0_ffn_shared_gate, L0_ffn_shared_up, L0_ffn_shared_down):

    def _L0_attn_ref(x, qkv_w, qkv_b, out_w, out_b):
        import jax, jax.numpy as jnp
        import numpy as np
        B, S, E, H, D = (4, 256, 128, 16, 64)

        def _large_negative_number(dtype):
            return jnp.asarray(-0.7 * jnp.finfo(dtype).max, dtype=dtype)
        qkv = jnp.einsum('bse,ehd->bshd', x, qkv_w) + qkv_b
        q, k, v = jnp.split(qkv, 3, axis=-1)
        logits = jnp.einsum('bqhd,bkhd->bhqk', q, k)
        logits = logits / jnp.sqrt(jnp.asarray(q.shape[-1], logits.dtype))
        mask = jnp.tril(jnp.ones((q.shape[1], q.shape[1]), dtype=jnp.bool_))
        logits = jnp.where(mask, logits, _large_negative_number(logits.dtype))
        probs = jax.nn.softmax(logits, axis=-1)
        attn = jnp.einsum('bhqk,bkhd->bqhd', probs, v)
        return jnp.einsum('bqhd,hde->bqe', attn, out_w) + out_b

    def _L0_ffn_ref(x, gate_w, expert_gate, expert_up, expert_down, shared_gate, shared_up, shared_down):
        import jax, jax.numpy as jnp
        import numpy as np
        TOP_K = 2

        def _ffn(x, gw, uw, dw):
            return jax.nn.silu(x @ gw.T) * (x @ uw.T) @ dw.T
        B, S, H = x.shape
        xf = x.reshape(-1, H)
        T = xf.shape[0]
        E = expert_gate.shape[0]
        shared = _ffn(xf, shared_gate, shared_up, shared_down)
        logits = xf @ gate_w.T
        probs = jax.nn.softmax(logits, axis=-1)
        topw, topi = jax.lax.top_k(probs, TOP_K)
        topw = topw / (topw.sum(-1, keepdims=True) + 1e-20)
        comb = jnp.zeros((T, E), xf.dtype).at[jnp.arange(T)[:, None], topi].add(topw)

        def body(acc, ws):
            gw, uw, dw, wcol = ws
            return (acc + _ffn(xf, gw, uw, dw) * wcol[:, None], None)
        routed, _ = jax.lax.scan(body, jnp.zeros_like(xf), (expert_gate, expert_up, expert_down, comb.T))
        return (shared + routed).reshape(B, S, H)
    x = L0_attn_x
    x = x + _L0_attn_ref(_layernorm(x, axis=-1), L0_attn_qkv_w, L0_attn_qkv_b, L0_attn_out_w, L0_attn_out_b)
    x = x + _L0_ffn_ref(_layernorm(x, axis=-1), L0_ffn_gate_w, L0_ffn_expert_gate, L0_ffn_expert_up, L0_ffn_expert_down, L0_ffn_shared_gate, L0_ffn_shared_up, L0_ffn_shared_down)
    return x

_drawn_inputs = setup_inputs


def setup_inputs(seed=0):
    import zlib

    import numpy as np

    out = dict(_drawn_inputs(seed))
    spreads = {'L0_attn_qkv_b': (0.0, 0.1), 'L0_attn_out_b': (0.0, 0.1)}
    factors = {'L0_ffn_gate_w': 8.0,
     'L0_ffn_expert_gate': 8.0,
     'L0_ffn_expert_up': 8.0,
     'L0_ffn_expert_down': 8.0,
     'L0_ffn_shared_gate': 5.962,
     'L0_ffn_shared_up': 5.923,
     'L0_ffn_shared_down': 5.963}
    for name, (base, spread) in spreads.items():
        noise = np.random.default_rng([zlib.crc32(name.encode()), seed]).standard_normal(out[name].shape)
        drawn = base * np.exp(spread * noise) if base else spread * noise
        out[name] = jnp.asarray(drawn.astype(out[name].dtype))
    for name, factor in factors.items():
        out[name] = (out[name] * factor).astype(out[name].dtype)
    return out
```

```python
from contextlib import ExitStack

import concourse.bass as bass
from concourse import mybir

F32, F32R = mybir.dt.float32, mybir.dt.float32r
F16, BF16, U32 = mybir.dt.float16, mybir.dt.bfloat16, mybir.dt.uint32
ALU, ACT = mybir.AluOpType, mybir.ActivationFunctionType
AX_X = mybir.AxisListType.X

P = 128
T = 2048
BLK = 512
NB = T // BLK
NT = T // P
H, D = 16, 64
PAIRS = H // 2
VW = 2 * D + 1
GROUPS = [(b, p) for b in range(NB) for p in range(2 * (b + 1))]
NG = len(GROUPS)
PRING, STRING, BGRING = 4, 2, 2
LAG = 2
EPS = 1e-5
NEG = -1.0e30
P_SCALE_LN = 2.772588722239781
F, FC = 352, 3
EXPERTS = 8
SHARED = EXPERTS
STEPS = NB * FC
HRING = 3
FLAG = 2


def sub_on_pool(n):
    return n % 5 in (1, 3)


def background(s, first, last):
    slots = [[] for _ in range(NG)]
    if not (last and s == 1):
        slots[0] += [("qk", 0), ("qk", 1)]
        slots[1] += [("qk", 2), ("qk", 3)]
        slots[2] += [("v", 0), ("v", 1)]
        slots[3] += [("v", 2), ("v", 3)]
        chunks = [("max", t, c) for t in range(NT) for c in range((t + 4) // 4)]
        where = list(range(4, 17))
        for k, task in enumerate(chunks):
            slots[where[k * len(where) // len(chunks)]].append(task)
        slots[17].append(("shift",))
    if s == 0 and not first:
        slots[3].append(("att_t", 3))
        slots[4].append(("att_y", 3))
    if s == 1:
        for b, n in ((0, 6), (1, 9), (2, 15)):
            slots[n].append(("att_t", b))
            slots[n + 1].append(("att_y", b))
    return slots


def count(slots):
    return sum(map(len, slots))


PROLOGUE = sum((s for s in background(1, False, False)), [])
PROLOGUE = [t for t in PROLOGUE if not t[0].startswith("att")]
N_FIRST = count(background(0, True, False)) + count(background(1, True, False))
N_LOOP = count(background(0, False, False)) + count(background(1, False, False))
N_LAST = count(background(0, False, True)) + count(background(1, False, True))
TAIL = [("att_t", 3), ("att_y", 3)]
BG_TOTAL = len(PROLOGUE) + N_FIRST + N_LOOP * (PAIRS - 2) + N_LAST + len(TAIL)
assert N_LOOP % BGRING == 0


def bg_base(i, first):
    return len(PROLOGUE) if first else (i - 1) * N_LOOP + (len(PROLOGUE) + N_FIRST)


def bg_bank(k_static):
    return k_static % BGRING


def wait(eng, sem, value):
    if not isinstance(value, int) or value > 0:
        eng.wait_ge(sem, value)


def layer_kernel(nc, x_t, qkv_w, qk_bias_in, v_bias, out_w, out_bias, gate_w_t, ffn_w, out_t):
    ctx = ExitStack()
    with ctx:
        def sb(name, shape, dtype):
            return ctx.enter_context(nc.sbuf_tensor(name, shape, dtype))

        def psum(name, shape, dtype):
            return ctx.enter_context(nc.psum_tensor(name, shape, dtype))

        def sem(name):
            return ctx.enter_context(nc.semaphore(name))

        res = sb("res", [P, T], F32)
        xn = sb("xn", [P, T], F32)
        xn_hi = sb("xn_hi", [P, T], F32R)
        xn_lo = sb("xn_lo", [P, T], F32R)
        q_hihi = [sb(f"q_hihi{s}", [P, T], F32R) for s in range(2)]
        k_hilo = [sb(f"k_hilo{s}", [P, T], F32R) for s in range(2)]
        q_lo_shift = [sb(f"q_lo_shift{s}", [P, T], F32R) for s in range(2)]
        k_hi_one = [sb(f"k_hi_one{s}", [P, T], F32R) for s in range(2)]
        v_parts = [sb(f"v_parts{s}", [P, NT, VW], F16) for s in range(2)]
        v32 = sb("v32", [P, 2, 4, D], F32)
        prob = sb("prob", [P, PRING, 2 * BLK], F32)
        p_hi = sb("p_hi", [P, PRING, 2 * BLK], F16)
        p_lo = sb("p_lo", [P, PRING, 2 * BLK], F16)
        row_max = sb("row_max", [P, NT, NB], F32)
        neg_max = sb("neg_max", [P, NT], F32)
        shift_row = sb("shift_row", [NT, P], F32R)
        attn = sb("attn", [P, NT, 2 * D], F32)
        pv_low = sb("pv_low", [P, 4, D], F32)
        pv_sum = sb("pv_sum", [P, 4, D], F32)
        rden = sb("rden", [P, 4, 1], F32)
        att_hi = sb("att_hi", [P, BLK], F32R)
        att_lo = sb("att_lo", [P, BLK], F32R)
        w_raw = [sb(f"w_raw{s}", [P, 3 * D], F32) for s in range(2)]
        w_hi = [sb(f"w_hi{s}", [P, 2 * D], F32R) for s in range(2)]
        w_lo = [sb(f"w_lo{s}", [P, 2 * D], F32R) for s in range(2)]
        qk_bias = [sb(f"qk_bias{s}", [P, 1], F32) for s in range(2)]
        vb = [sb(f"vb{s}", [P, D], F32) for s in range(2)]
        wo_raw = sb("wo_raw", [P, P], F32)
        wo_hi = sb("wo_hi", [P, P], F32R)
        wo_lo = sb("wo_lo", [P, P], F32R)
        obias = sb("obias", [P, 1], F32)
        ones_mean = sb("ones_mean", [P, P], F32)
        ident = sb("ident", [P, P], F32)
        ident_bf = sb("ident_bf", [P, P], BF16)
        mask_rows = sb("mask_rows", [P, P], BF16)
        mask_cols = sb("mask_cols", [P, P], BF16)
        eps = sb("eps", [P, 1], F32)
        p_bias = sb("p_bias", [P, 1], F32)
        gate_w = sb("gate_w", [P, EXPERTS], F32)
        lg = sb("lg", [P, NT, EXPERTS], F32)
        lg_max = sb("lg_max", [P, NT, 1], F32)
        pr = sb("pr", [P, NT, EXPERTS], F32)
        pr_sum = sb("pr_sum", [P, NT, 1], F32)
        top = sb("top", [P, NT, 8], F32)
        top_at = sb("top_at", [P, NT, 8], U32)
        top_atf = sb("top_atf", [P, NT, 2], F32)
        top_w = sb("top_w", [P, NT, 2], F32)
        wsum = sb("wsum", [P, NT, 1], F32)
        iota8 = sb("iota8", [P, 1, EXPERTS], F32)
        hot = sb("hot", [P, 2, NT, EXPERTS], F32)
        comb = sb("comb", [P, NT, EXPERTS], F32)
        comb_t = sb("comb_t", [EXPERTS, T], F32)
        w_tok = sb("w_tok", [P, T], F32)
        xw32 = sb("xw32", [P, 2, BLK], F32)
        e_raw = [sb(f"e_raw{s}", [P, 3 * FC * P], F32) for s in range(2)]
        h_hi = sb("h_hi", [P, HRING, BLK], F32R)
        h_lo = sb("h_lo", [P, HRING, BLK], F32R)
        sq = prob[:, 0:2, :].rearrange("p a b -> p (a b)")
        std = prob[:, 2:4, :].rearrange("p a b -> p (a b)")
        pflat = prob[:, :, :].rearrange("p a b -> p (a b)")
        silu = [pflat[:, k * BLK:(k + 1) * BLK] for k in range(HRING)]
        h32 = [pflat[:, (HRING + k) * BLK:(HRING + k + 1) * BLK] for k in range(HRING)]
        e_hi, e_lo = k_hi_one, q_lo_shift
        xw_hi, xw_lo = q_hihi, k_hilo
        comb_dram = nc.dram_tensor("comb_dram", [EXPERTS, T], F32, kind="Internal").ap()

        st = psum("st", [P, STRING, 2, BLK], F32)
        bg = psum("bg", [P, BGRING, BLK], F32)
        pv = psum("pv", [P, 2, BLK], F32)
        pv4 = pv[:, :, 0:2 * VW].rearrange("p a (j c) -> p a j c", c=VW)
        mean_bank = [st[:, b // 2, b % 2, :] for b in range(NB)]
        y_bank = [bg[:, 0, :], bg[:, 1, :], pv[:, 0, :], pv[:, 1, :]]

        x_landed, small_landed = sem("x_landed"), sem("small_landed")
        head_w_landed = [sem(f"head_w_landed{s}") for s in range(2)]
        wo_landed, wo_hi_ready, wo_lo_ready = sem("wo_landed"), sem("wo_hi_ready"), sem("wo_lo_ready")
        w_hi_ready, w_lo_ready = sem("w_hi_ready"), sem("w_lo_ready")
        consts, pool_self = sem("consts"), sem("pool_self")
        ones_ready = sem("ones_ready")
        ln_mean, ln_centered, ln_sq, ln_var = sem("ln_mean"), sem("ln_centered"), sem("ln_sq"), sem("ln_var")
        ln_std, ln_rstd, xn_ready = sem("ln_std"), sem("ln_rstd"), sem("xn_ready")
        xn_hi_ready, xn_lo_ready = sem("xn_hi_ready"), sem("xn_lo_ready")
        res_ready = sem("res_ready")
        st_ready, exp_done = sem("st_ready"), sem("exp_done")
        lo_dve, lo_pool = sem("lo_dve"), sem("lo_pool")
        p_used, pv_low_ready, pv_drained = sem("p_used"), sem("pv_low_ready"), sem("pv_drained")
        evac_self = sem("evac_self")
        bg_ready, bg_drained = sem("bg_ready"), sem("bg_drained")
        qk_hi_ready, qk_dup_landed = sem("qk_hi_ready"), sem("qk_dup_landed")
        v_hi_ready, v_lo_ready = sem("v_hi_ready"), sem("v_lo_ready")
        neg_max_ready, shift_landed = sem("neg_max_ready"), sem("shift_landed")
        att_hi_ready = sem("att_hi_ready")
        logits_ready, router_max, router, router_exp, comb_ready = sem("logits_ready"), sem("router_max"), sem("router"), sem("router_exp"), sem("comb_ready")
        comb_t_ready, comb_t_copied, comb_stored = sem("comb_t_ready"), sem("comb_t_copied"), sem("comb_stored")
        e_landed = [sem(f"e_landed{s}") for s in range(2)]
        w_tok_landed, xw_ready, xw_hi_ready, xw_lo_ready = sem("w_tok_landed"), sem("xw_ready"), sem("xw_hi_ready"), sem("xw_lo_ready")
        e_hi_ready, e_lo_ready = sem("e_hi_ready"), sem("e_lo_ready")
        gu_ready, silu_done, h_ready = sem("gu_ready"), sem("silu_done"), sem("h_ready")
        h_hi_ready, h_lo_ready, down_done = sem("h_hi_ready"), sem("h_lo_ready"), sem("down_done")
        out_copied_act, out_copied_dve, out_stored = sem("out_copied_act"), sem("out_copied_dve"), sem("out_stored")

        N_CONST = 13
        pool_per_head = sum(sub_on_pool(n) for n in range(NG))
        dve_per_head = NG - pool_per_head

        def lo_sem(G_head, n):
            if sub_on_pool(n):
                return lo_pool, G_head * pool_per_head + sum(sub_on_pool(k) for k in range(n + 1))
            return lo_dve, G_head * dve_per_head + sum(not sub_on_pool(k) for k in range(n + 1))

        def columns(n):
            b, p = GROUPS[n]
            return (256 if p == 2 * b + 1 else 0), BLK

        def ends_block(n):
            b, p = GROUPS[n]
            return p == 2 * b + 1

        def blk(b):
            return slice(b * BLK, (b + 1) * BLK)

        def tile(t):
            return slice(t * P, (t + 1) * P)

        def max_width(t, c):
            return min(BLK, P * (t + 1) - BLK * c)

        def v_quad(slot, q, lo, hi):
            return v_parts[slot][:, 4 * q:4 * q + 4, lo:hi]

        def pairs(eng, body):
            body(0, True, False)
            with eng.Fori(1, PAIRS - 1) as i:
                body(i, False, False)
            body(PAIRS - 1, False, True)

        def passes(eng, body):
            body(0, 1, True, False)
            with eng.Fori(0, 3) as j:
                body(j * 2 + 1, 0, False, False)
                body(j * 2 + 2, 1, False, False)
            body(7, 0, False, False)
            body(8, 1, False, True)

        block = ctx.enter_context(nc.Block())

        @block.sync
        def _(sp):
            for b in range(NB):
                sp.dma_start(res[:, blk(b)], x_t[:, blk(b)]).then_inc(x_landed, 16)
            sp.dma_start(obias[:], out_bias).then_inc(small_landed, 16)
            sp.dma_start(gate_w[:], gate_w_t).then_inc(small_landed, 16)

            def head_weights(h, s):
                hs = bass.ds(h, 1)
                sp.dma_start(w_raw[s][:], qkv_w[:, hs, :].rearrange("e h d -> e (h d)")).then_inc(head_w_landed[s], 16)
                sp.dma_start(qk_bias[s][:], qk_bias_in[hs, :, :].rearrange("o p c -> (o p) c")).then_inc(head_w_landed[s], 16)
                sp.dma_start(vb[s][:], v_bias[hs, :].broadcast_to([P, D])).then_inc(head_w_landed[s], 16)

            def dup_and_shift(h, s, shift_count):
                sp.wait_ge(qk_hi_ready, h * NB + NB)
                sp.dma_start(q_hihi[s][D:P, :].bitcast(F32), q_hihi[s][0:D, :].bitcast(F32)).then_inc(qk_dup_landed, 16)
                sp.dma_start(k_hi_one[s][0:D, :].bitcast(F32), k_hilo[s][0:D, :].bitcast(F32)).then_inc(qk_dup_landed, 16)
                sp.wait_ge(bg_drained, shift_count)
                sp.dma_start(q_lo_shift[s][D:D + 1, :].bitcast(F32),
                             shift_row[:, :].bitcast(F32)).then_inc(shift_landed, 16)

            head_weights(0, 0)
            head_weights(1, 1)
            dup_and_shift(0, 0, len(PROLOGUE))

            def body(i, first, last):
                base = bg_base(i, first)
                for s in range(2):
                    h = i * 2 + s
                    tasks = sum(background(s, first, last), [])
                    sp.wait_ge(st_ready, h * NG + 1)
                    if s == 0:
                        wait(sp, wo_lo_ready, i)
                        sp.dma_start(wo_raw[:], out_w[bass.ds(i * P, P), :]).then_inc(wo_landed, 16)
                    if not last:
                        head_weights(h + 2, s)
                    if not (last and s == 1):
                        dup_and_shift(h + 1, 1 - s, base + tasks.index(("shift",)) + 1)
                    base = base + len(tasks)

            pairs(sp, body)

            def expert_weights(p, s, expert):
                sp.dma_start(e_raw[s][:], ffn_w[bass.ds(expert, 1), :, :].rearrange("o p w -> (o p) w")
                             ).then_inc(e_landed[s], 16)

            expert_weights(0, 1, SHARED)
            expert_weights(1, 0, 0)
            sp.wait_ge(comb_t_copied, 4)
            sp.dma_start(comb_dram, comb_t[:]).then_inc(comb_stored, 16)
            sp.wait_ge(comb_stored, 16)

            def body(p, s, first, last):
                if last:
                    return
                if not first:
                    sp.wait_ge(xw_ready, p * NB)
                sp.dma_start(w_tok[:], comb_dram[bass.ds(p, 1), :].broadcast_to([P, T])
                             ).then_inc(w_tok_landed, 16)
                if isinstance(p, int) and p >= 7:
                    return
                sp.wait_ge(e_hi_ready, p + 1)
                sp.wait_ge(e_lo_ready, p + 1)
                expert_weights(p + 2, s, p + 1)

            passes(sp, body)
            for b in range(NB):
                done = (out_copied_act, out_copied_dve)[b % 2]
                sp.wait_ge(done, b // 2 + 1)
                sp.dma_start(out_t[:, blk(b)], xn[:, blk(b)]).then_inc(out_stored, 16)
            sp.wait_ge(out_stored, 16 * NB)

        @block.gpsimd
        def _(pool):
            nc.gpsimd.memset(ones_mean[:], 1.0 / P).then_inc(ones_ready, 1)
            nc.gpsimd.memset(eps[:], EPS).then_inc(consts, 1)
            nc.gpsimd.memset(p_bias[:], P_SCALE_LN).then_inc(consts, 1)
            nc.gpsimd.memset(ident[:], 0.0).then_inc(pool_self, 1)
            nc.gpsimd.memset(ident_bf[:], 0.0).then_inc(pool_self, 1)
            nc.gpsimd.memset(mask_rows[:], 0.0).then_inc(pool_self, 1)
            nc.gpsimd.memset(mask_cols[:], 0.0).then_inc(pool_self, 1)
            pool.wait_ge(pool_self, 4)
            for i in (ident, ident_bf):
                nc.gpsimd.affine_select(out=i[:], in_=i[:], compare_op=ALU.not_equal, fill=1.0, base=0,
                                        pattern=[[-1, P]], channel_multiplier=1).then_inc(consts, 1)
            nc.gpsimd.affine_select(out=mask_rows[:], in_=mask_rows[:], compare_op=ALU.is_ge, fill=NEG, base=0,
                                    pattern=[[-1, P]], channel_multiplier=1).then_inc(consts, 1)
            nc.gpsimd.affine_select(out=mask_cols[:], in_=mask_cols[:], compare_op=ALU.is_ge, fill=NEG, base=0,
                                    pattern=[[1, P]], channel_multiplier=-1).then_inc(consts, 1)
            for s in range(2):
                nc.gpsimd.memset(v_parts[s][:, :, D:D + 1], 1.0).then_inc(consts, 1)
            nc.gpsimd.memset(row_max[:], -3.0e38).then_inc(consts, 1)
            nc.gpsimd.iota(iota8[:, 0, :], pattern=[[1, EXPERTS]], base=0, channel_multiplier=0,
                           allow_small_or_imprecise_dtypes=True).then_inc(consts, 1)
            nc.gpsimd.memset(pv_sum[:], 0.0).then_inc(consts, 1)

            def v_low(h, s, q):
                pool.wait_ge(v_hi_ready, h * 4 + q + 1)
                nc.gpsimd.tensor_tensor(v_quad(s, q, D + 1, VW), v32[:, q % 2], v_quad(s, q, 0, D),
                                        ALU.subtract).then_inc(v_lo_ready, 1)

            for q in range(4):
                v_low(0, 0, q)

            def p_low(h, n):
                G = h * NG + n
                lo, hi = columns(n)
                pool.wait_ge(exp_done, G + 1)
                ring = n % PRING
                a = prob[:, ring].rearrange("p (k c) -> p k c", k=2)[:, :, lo:hi]
                b = p_hi[:, ring].rearrange("p (k c) -> p k c", k=2)[:, :, lo:hi]
                o = p_lo[:, ring].rearrange("p (k c) -> p k c", k=2)[:, :, lo:hi]
                nc.gpsimd.tensor_tensor(o, a, b, ALU.subtract).then_inc(lo_pool, 1)

            def body(i, first, last):
                for s in range(2):
                    h = i * 2 + s
                    slots = background(s, first, last)
                    for n in range(NG):
                        for task in slots[n]:
                            if task[0] == "v":
                                v_low(h + 1, 1 - s, task[1])
                        if sub_on_pool(n):
                            p_low(h, n)

            pairs(pool, body)

        @block.scalar
        def _(act):
            def layer_norm(turn):
                for b in range(NB):
                    act.wait_ge(ln_centered, turn * NB + b + 1)
                    nc.scalar.activation(sq[:, blk(b)], xn[:, blk(b)], ACT.Square).then_inc(ln_sq, 1)
                for b in range(NB):
                    act.wait_ge(ln_var, turn * NB + b + 1)
                    nc.scalar.activation(std[:, blk(b)], y_bank[b], ACT.Sqrt, bias=eps[:]).then_inc(ln_std, 1)
                for b in range(NB):
                    act.wait_ge(xn_ready, turn * NB + b + 1)
                    nc.scalar.copy(xn_hi[:, blk(b)], xn[:, blk(b)]).then_inc(xn_hi_ready, 1)

            def split_head_weights(h, s, landed):
                act.wait_ge(head_w_landed[s], landed)
                nc.scalar.copy(w_hi[s][:], w_raw[s][:, 0:2 * D]).then_inc(w_hi_ready, 1)

            def background_task(task, k, bank, h, s):
                if task[0] == "qk":
                    b = task[1]
                    act.wait_ge(bg_ready, k + 1)
                    nc.scalar.activation(q_hihi[s][0:D, blk(b)], bg[0:D, bank], ACT.Identity,
                                         bias=qk_bias[s][0:D, :])
                    nc.scalar.activation(k_hilo[s][0:D, blk(b)], bg[D:P, bank], ACT.Identity,
                                         bias=qk_bias[s][D:P, :]).then_inc(qk_hi_ready, 1)
                elif task[0] == "v":
                    q = task[1]
                    act.wait_ge(bg_drained, k + 1)
                    nc.scalar.copy(v_quad(s, q, 0, D), v32[:, q % 2]).then_inc(v_hi_ready, 1)
                elif task[0] == "att_t":
                    act.wait_ge(bg_ready, k + 1)
                    nc.scalar.copy(att_hi[:], bg[:, bank]).then_inc(att_hi_ready, 1)

            def exps(h, n):
                G = h * NG + n
                lo, hi = columns(n)
                act.wait_ge(st_ready, G + 1)
                wait(act, p_used, G - PRING + 1)
                src = st[:, n % STRING, :, lo:hi]
                o32 = prob[:, n % PRING].rearrange("p (k c) -> p k c", k=2)[:, :, lo:hi]
                o16 = p_hi[:, n % PRING].rearrange("p (k c) -> p k c", k=2)[:, :, lo:hi]
                nc.scalar.activation(o32, src, ACT.Exp, bias=p_bias[:], scale=D ** -0.5)
                nc.scalar.activation(o16, src, ACT.Exp, bias=p_bias[:], scale=D ** -0.5).then_inc(exp_done, 1)

            def evacuate(h, n):
                act.wait_ge(p_used, h * NG + n + 1)
                nc.scalar.copy(pv_low[:].rearrange("p (a j) d -> p a j d", a=2),
                               pv4[:, :, :, D + 1:VW]).then_inc(pv_low_ready, 1)

            act.wait_ge(consts, N_CONST)
            layer_norm(0)
            split_head_weights(0, 0, 48)
            split_head_weights(1, 1, 48)
            for k, task in enumerate(PROLOGUE):
                background_task(task, k, bg_bank(k), 0, 0)

            def body(i, first, last):
                base, at = bg_base(i, first), bg_base(0 if first else 1, first)
                for s in range(2):
                    h = i * 2 + s
                    slots = background(s, first, last)
                    for n in range(NG):
                        m = (n - LAG - 1) % NG
                        if ends_block(m) and not (first and s == 0 and m > n):
                            evacuate(h if m < n else h - 1, m)
                        exps(h, n)
                        for task in slots[n]:
                            background_task(task, base, bg_bank(at), h + 1, 1 - s)
                            base, at = base + 1, at + 1
                        if n == 10 and not last:
                            split_head_weights(h + 2, s, (i + 2) * 48)
                        if n == 10 and s == 0:
                            act.wait_ge(wo_landed, i * 16 + 16)
                            wait(act, bg_drained, base)
                            nc.scalar.copy(wo_hi[:], wo_raw[:]).then_inc(wo_hi_ready, 1)

            pairs(act, body)
            evacuate(H - 1, NG - 1)
            k = BG_TOTAL - 2
            background_task(TAIL[0], k, bg_bank(k), None, None)
            layer_norm(1)

            act.wait_ge(router, 1)
            nc.scalar.activation(pr[:], lg[:], ACT.Exp).then_inc(router_exp, 1)
            for b in range(NB):
                act.wait_ge(comb_t_ready, 1)
                nc.scalar.copy(comb_t[:, blk(b)], mean_bank[b][0:EXPERTS, :]).then_inc(comb_t_copied, 1)

            def expert_hi(p, s, landed):
                act.wait_ge(e_landed[s], landed)
                nc.scalar.copy(e_hi[s][:, 0:3 * FC * P], e_raw[s][:]).then_inc(e_hi_ready, 1)

            def hidden_hi(Q, q):
                act.wait_ge(h_ready, Q + 1)
                wait(act, down_done, Q - HRING + 1)
                nc.scalar.copy(h_hi[:, q % HRING], h32[q % HRING]).then_inc(h_hi_ready, 1)

            expert_hi(0, 1, 16)

            def body(p, s, first, last):
                for q in range(STEPS):
                    Q = p * STEPS + q
                    act.wait_ge(gu_ready, Q + 1)
                    nc.scalar.activation(silu[q % HRING], st[:, q % 2, 0, :], ACT.Silu).then_inc(silu_done, 1)
                    if not (first and q == 0):
                        hidden_hi(Q - 1, (q - 1) % STEPS)
                    if last:
                        continue
                    if q == 2:
                        wait(act, down_done, p * STEPS)
                        expert_hi(p + 1, 1 - s, e_count(p, s))
                    if 3 <= q < 3 + NB:
                        b = q - 3
                        act.wait_ge(xw_ready, p * NB + b + 1)
                        nc.scalar.copy(xw_hi[1 - s][:, blk(b)], xw32[:, b % 2]).then_inc(xw_hi_ready, 1)

            def e_count(p, s):
                return (p + 1) * 8 + 16 if s == 0 else (p + 2) * 8

            passes(act, body)
            hidden_hi(9 * STEPS - 1, STEPS - 1)
            for b in (0, 2):
                act.wait_ge(down_done, 8 * STEPS + FC * (b + 1))
                nc.scalar.copy(xn[:, blk(b)], y_bank[b]).then_inc(out_copied_act, 1)

        @block.vector
        def _(dve):
            def layer_norm(turn):
                for b in range(NB):
                    dve.wait_ge(ln_mean, turn * NB + b + 1)
                    nc.vector.tensor_tensor(xn[:, blk(b)], res[:, blk(b)], mean_bank[b], ALU.subtract
                                            ).then_inc(ln_centered, 1)
                for b in range(NB):
                    dve.wait_ge(ln_std, turn * NB + b + 1)
                    nc.vector.reciprocal(std[:, blk(b)], std[:, blk(b)]).then_inc(ln_rstd, 1)
                    dve.wait_ge(ln_rstd, turn * NB + b + 1)
                    nc.vector.tensor_tensor(xn[:, blk(b)], xn[:, blk(b)], std[:, blk(b)], ALU.mult
                                            ).then_inc(xn_ready, 1)
                for b in range(NB):
                    dve.wait_ge(xn_hi_ready, turn * NB + b + 1)
                    nc.vector.tensor_tensor(xn_lo[:, blk(b)], xn[:, blk(b)], xn_hi[:, blk(b)], ALU.subtract
                                            ).then_inc(xn_lo_ready, 1)

            def split_head_weights(h, s):
                dve.wait_ge(w_hi_ready, h + 1)
                nc.vector.tensor_tensor(w_lo[s][:], w_raw[s][:, 0:2 * D], w_hi[s][:], ALU.subtract
                                        ).then_inc(w_lo_ready, 1)

            def background_task(task, k, bank, h, s, maxes, att):
                dve.wait_ge(bg_ready, k + 1)
                if task[0] == "qk":
                    b = task[1]
                    dve.wait_ge(qk_hi_ready, h * NB + b + 1)
                    nc.vector.scalar_tensor_tensor(out=q_lo_shift[s][0:D, blk(b)], in0=bg[0:D, bank],
                                                   scalar=qk_bias[s][0:D, :], in1=q_hihi[s][0:D, blk(b)],
                                                   op0=ALU.add, op1=ALU.subtract)
                    nc.vector.scalar_tensor_tensor(out=k_hilo[s][D:P, blk(b)], in0=bg[D:P, bank],
                                                   scalar=qk_bias[s][D:P, :], in1=k_hilo[s][0:D, blk(b)],
                                                   op0=ALU.add, op1=ALU.subtract).then_inc(bg_drained, 1)
                elif task[0] == "v":
                    q = task[1]
                    wait(dve, v_lo_ready, h * 4 + q - 1)
                    nc.vector.tensor_tensor(v32[:, q % 2], bg[:, bank].rearrange("p (r c) -> p r c", r=4)[:, :, D:P],
                                            vb[s][:].unsqueeze(1).broadcast_to([P, 4, D]), ALU.add
                                            ).then_inc(bg_drained, 1)
                elif task[0] == "max":
                    t, c = task[1:]
                    nc.vector.tensor_reduce(row_max[:, t, c:c + 1], bg[:, bank, 0:max_width(t, c)], AX_X,
                                            ALU.max).then_inc(bg_drained, 1)
                    if (t, c) == (NT - 1, NB - 1):
                        dve.wait_ge(bg_drained, k + 1)
                        nc.vector.tensor_reduce(neg_max[:], row_max[:], AX_X, ALU.max, negate=True
                                                ).then_inc(neg_max_ready, 1)
                elif task[0] == "shift":
                    wait(dve, shift_landed, h * 16)
                    nc.vector.tensor_copy(shift_row[:], bg[0:NT, bank, 0:P]).then_inc(bg_drained, 1)
                elif task[0] == "att_t":
                    dve.wait_ge(att_hi_ready, att * NB + task[1] + 1)
                    nc.vector.tensor_tensor(att_lo[:], bg[:, bank], att_hi[:], ALU.subtract
                                            ).then_inc(bg_drained, 1)
                elif task[0] == "att_y":
                    b = task[1]
                    nc.vector.tensor_tensor(res[:, blk(b)], res[:, blk(b)], bg[:, bank], ALU.add
                                            ).then_inc(bg_drained, 1)

            def p_low(h, n):
                G = h * NG + n
                lo, hi = columns(n)
                dve.wait_ge(exp_done, G + 1)
                ring = n % PRING
                a = prob[:, ring].rearrange("p (k c) -> p k c", k=2)[:, :, lo:hi]
                b = p_hi[:, ring].rearrange("p (k c) -> p k c", k=2)[:, :, lo:hi]
                o = p_lo[:, ring].rearrange("p (k c) -> p k c", k=2)[:, :, lo:hi]
                nc.vector.tensor_tensor(o, a, b, ALU.subtract).then_inc(lo_dve, 1)

            def evacuate(h, n, s):
                b = GROUPS[n][0]
                B = h * NB + b
                dve.wait_ge(pv_low_ready, B + 1)
                nc.vector.reciprocal(rden[:].rearrange("p (a j) o -> p a j o", a=2), pv4[:, :, :, D:D + 1])
                nc.vector.tensor_tensor(pv_sum[:].rearrange("p (a j) d -> p a j d", a=2), pv4[:, :, :, 0:D],
                                        pv_low[:].rearrange("p (a j) d -> p a j d", a=2), ALU.add
                                        ).then_inc(evac_self, 1)
                dve.wait_ge(evac_self, B + 1)
                nc.vector.tensor_tensor(attn[:, 4 * b:4 * b + 4, s * D:(s + 1) * D], pv_sum[:],
                                        rden[:].broadcast_to([P, 4, D]), ALU.mult).then_inc(pv_drained, 1)

            for s in range(2):
                nc.vector.memset(k_hi_one[s][D:D + 1, :].bitcast(F32), 1.0).then_inc(consts, 1)
            dve.wait_ge(x_landed, 16 * NB)
            layer_norm(0)
            dve.wait_ge(small_landed, 32)
            dve.wait_ge(consts, N_CONST)
            nc.vector.tensor_scalar(res[:], res[:], obias[:, 0:1], None, ALU.add).then_inc(res_ready, 1)
            dve.wait_ge(res_ready, 1)
            split_head_weights(0, 0)
            split_head_weights(1, 1)
            for k, task in enumerate(PROLOGUE):
                background_task(task, k, bg_bank(k), 0, 0, None, None)

            def body(i, first, last):
                base, at = bg_base(i, first), bg_base(0 if first else 1, first)
                for s in range(2):
                    h = i * 2 + s
                    slots = background(s, first, last)
                    for n in range(NG):
                        m = (n - 1) % NG
                        if not sub_on_pool(m) and not (first and s == 0 and n == 0):
                            p_low(h if n else h - 1, m)
                        m = (n - LAG - 1) % NG
                        if ends_block(m) and not (first and s == 0 and m > n):
                            evacuate(h if m < n else h - 1, m, s if m < n else 1 - s)
                        for task in slots[n]:
                            background_task(task, base, bg_bank(at), h + 1, 1 - s, None, i if s else i - 1)
                            base, at = base + 1, at + 1
                        if n == 10 and not last:
                            split_head_weights(h + 2, s)
                        if n == 10 and s == 0:
                            dve.wait_ge(wo_hi_ready, i + 1)
                            nc.vector.tensor_tensor(wo_lo[:], wo_raw[:], wo_hi[:], ALU.subtract
                                                    ).then_inc(wo_lo_ready, 1)

            pairs(dve, body)
            if not sub_on_pool(NG - 1):
                p_low(H - 1, NG - 1)
            evacuate(H - 1, NG - 1, 1)
            for k, task in zip((BG_TOTAL - 2, BG_TOTAL - 1), TAIL):
                background_task(task, k, bg_bank(k), None, None, None, PAIRS - 1)
            layer_norm(1)

            steps = [0]

            def own(ins):
                steps[0] += 1
                ins.then_inc(router, 1)
                dve.wait_ge(router, steps[0])

            dve.wait_ge(logits_ready, 1)
            logits = st[:, 0, 0, 0:NT * EXPERTS].rearrange("p (t e) -> p t e", e=EXPERTS)
            nc.vector.tensor_reduce(lg_max[:, :, 0], logits, AX_X, ALU.max).then_inc(router_max, 1)
            dve.wait_ge(router_max, 1)
            own(nc.vector.tensor_tensor(lg[:], logits, lg_max[:].broadcast_to([P, NT, EXPERTS]), ALU.subtract))
            dve.wait_ge(router_exp, 1)
            own(nc.vector.tensor_reduce(pr_sum[:, :, 0], pr[:], AX_X, ALU.add))
            own(nc.vector.reciprocal(pr_sum[:], pr_sum[:]))
            own(nc.vector.tensor_tensor(pr[:], pr[:], pr_sum[:].broadcast_to([P, NT, EXPERTS]), ALU.mult))
            for t in range(NT):
                last_max = nc.vector.max(top[:, t, :], pr[:, t, :])
            own(last_max)
            for t in range(NT):
                last_at = nc.vector.max_index(top_at[:, t, :], top[:, t, :], pr[:, t, :])
            own(last_at)
            own(nc.vector.tensor_copy(top_atf[:], top_at[:, :, 0:2]))
            own(nc.vector.scalar_tensor_tensor(out=wsum[:, :, 0], in0=top[:, :, 0], scalar=1e-20, in1=top[:, :, 1],
                                               op0=ALU.add, op1=ALU.add))
            own(nc.vector.reciprocal(wsum[:], wsum[:]))
            own(nc.vector.tensor_tensor(top_w[:], top[:, :, 0:2], wsum[:].broadcast_to([P, NT, 2]), ALU.mult))
            for r in range(2):
                own(nc.vector.tensor_tensor(hot[:, r], iota8[:].broadcast_to([P, NT, EXPERTS]),
                                            top_atf[:, :, r:r + 1].broadcast_to([P, NT, EXPERTS]), ALU.is_equal))
                own(nc.vector.tensor_tensor(hot[:, r], hot[:, r],
                                            top_w[:, :, r:r + 1].broadcast_to([P, NT, EXPERTS]), ALU.mult))
            nc.vector.tensor_tensor(comb[:], hot[:, 0], hot[:, 1], ALU.add).then_inc(comb_ready, 1)

            def expert_lo(p, s):
                dve.wait_ge(e_hi_ready, p + 1)
                nc.vector.tensor_tensor(e_lo[s][:, 0:3 * FC * P], e_raw[s][:], e_hi[s][:, 0:3 * FC * P],
                                        ALU.subtract).then_inc(e_lo_ready, 1)

            def hidden_lo(Q, q):
                dve.wait_ge(h_hi_ready, Q + 1)
                nc.vector.tensor_tensor(h_lo[:, q % HRING], h32[q % HRING], h_hi[:, q % HRING],
                                        ALU.subtract).then_inc(h_lo_ready, 1)

            def weighted_input(p, b):
                if b == 0:
                    dve.wait_ge(w_tok_landed, p * 16 + 16)
                wait(dve, xw_lo_ready, p * NB + b - 1)
                nc.vector.tensor_tensor(xw32[:, b % 2], xn[:, blk(b)], w_tok[:, blk(b)], ALU.mult
                                        ).then_inc(xw_ready, 1)

            def weighted_lo(p, s, b):
                dve.wait_ge(xw_hi_ready, p * NB + b + 1)
                nc.vector.tensor_tensor(xw_lo[s][:, blk(b)], xw32[:, b % 2], xw_hi[s][:, blk(b)], ALU.subtract
                                        ).then_inc(xw_lo_ready, 1)

            expert_lo(0, 1)

            def body(p, s, first, last):
                for q in range(STEPS):
                    Q = p * STEPS + q
                    dve.wait_ge(silu_done, Q + 1)
                    nc.vector.tensor_tensor(h32[q % HRING], silu[q % HRING], st[:, q % 2, 1, :], ALU.mult
                                            ).then_inc(h_ready, 1)
                    if not (first and q == 0):
                        hidden_lo(Q - 1, (q - 1) % STEPS)
                    if last:
                        continue
                    if q == 3:
                        expert_lo(p + 1, 1 - s)
                    if 4 <= q < 4 + NB:
                        weighted_lo(p, 1 - s, q - 4)
                    if 2 <= q < 2 + NB:
                        weighted_input(p, q - 2)

            passes(dve, body)
            hidden_lo(9 * STEPS - 1, STEPS - 1)
            for b in (1, 3):
                dve.wait_ge(down_done, 8 * STEPS + FC * (b + 1))
                nc.vector.tensor_copy(xn[:, blk(b)], y_bank[b]).then_inc(out_copied_dve, 1)

        @block.tensor
        def _(pe):
            def mm3(out, w_hi_ap, w_lo_ap, x_hi_ap, x_lo_ap, start, stop, skip=False):
                nc.tensor.matmul(out, w_hi_ap, x_hi_ap, start=start, stop=False, skip_group_check=skip)
                nc.tensor.matmul(out, w_hi_ap, x_lo_ap, start=False, stop=False, skip_group_check=skip)
                return nc.tensor.matmul(out, w_lo_ap, x_hi_ap, start=False, stop=stop, skip_group_check=skip)

            def layer_norm(turn):
                for b in range(NB):
                    if turn == 0:
                        pe.wait_ge(x_landed, 16 * NB)
                    nc.tensor.matmul(mean_bank[b], ones_mean[:], res[:, blk(b)], start=True, stop=True
                                     ).then_inc(ln_mean, 1)
                for b in range(NB):
                    pe.wait_ge(ln_sq, turn * NB + b + 1)
                    nc.tensor.matmul(y_bank[b], ones_mean[:], sq[:, blk(b)], start=True, stop=True
                                     ).then_inc(ln_var, 1)

            def background_task(task, k, bank, h, s, pair):
                wait(pe, bg_drained, k - BGRING + 1)
                if task[0] == "qk":
                    b = task[1]
                    if b == 0:
                        pe.wait_ge(w_lo_ready, h + 1)
                    mm3(bg[:, bank], w_hi[s][:], w_lo[s][:], xn_hi[:, blk(b)], xn_lo[:, blk(b)], True, True
                        ).then_inc(bg_ready, 1)
                elif task[0] == "v":
                    for r in range(4):
                        mm = nc.tensor.matmul(bg[:, bank, tile(r)], xn[:, tile(4 * task[1] + r)],
                                              w_raw[s][:, D:3 * D], start=True, stop=True)
                    mm.then_inc(bg_ready, 1)
                elif task[0] == "max":
                    t, c = task[1:]
                    if (t, c) == (0, 0):
                        pe.wait_ge(qk_dup_landed, h * 32 + 32)
                    width = max_width(t, c)
                    wide = max(256, width)
                    diagonal = c == t // 4
                    mm = nc.tensor.matmul(bg[:, bank, 0:wide], q_hihi[s][:, tile(t)],
                                          k_hilo[s][:, c * BLK:c * BLK + wide], start=True, stop=not diagonal)
                    if diagonal:
                        mm = nc.tensor.matmul(bg[:, bank, width - P:width], ident_bf[:], mask_rows[:],
                                              start=False, stop=True)
                    mm.then_inc(bg_ready, 1)
                elif task[0] == "shift":
                    pe.wait_ge(neg_max_ready, h + 1)
                    nc.tensor.transpose(bg[0:NT, bank, 0:P], neg_max[:], ident[:]).then_inc(bg_ready, 1)
                elif task[0] == "att_t":
                    b = task[1]
                    pe.wait_ge(pv_drained, (pair * 2 + 1) * NB + b + 1)
                    for r in range(4):
                        mm = nc.tensor.transpose(bg[:, bank, tile(r)], attn[:, 4 * b + r, :], ident[:])
                    mm.then_inc(bg_ready, 1)
                elif task[0] == "att_y":
                    pe.wait_ge(wo_lo_ready, pair + 1)
                    pe.wait_ge(bg_drained, k)
                    mm3(bg[:, bank], wo_hi[:], wo_lo[:], att_hi[:], att_lo[:], True, True).then_inc(bg_ready, 1)

            def scores(h, s, n):
                G = h * NG + n
                b, p = GROUPS[n]
                lo, hi = columns(n)
                wait(pe, exp_done, G - STRING + 1)
                if n == 0:
                    pe.wait_ge(shift_landed, h * 16 + 16)
                for k in range(2):
                    kt = 2 * p + k
                    out = st[:, n % STRING, k, lo:hi]
                    q = slice(b * BLK + lo, b * BLK + hi)
                    diagonal = kt >= 4 * b
                    nc.tensor.matmul(out, k_hilo[s][:, tile(kt)], q_hihi[s][:, q], start=True, stop=False)
                    mm = nc.tensor.matmul(out, k_hi_one[s][0:D + 1, tile(kt)], q_lo_shift[s][0:D + 1, q],
                                          start=False, stop=not diagonal)
                    if diagonal:
                        j = kt - 4 * b
                        mm = nc.tensor.matmul(st[:, n % STRING, k, tile(j)], ident_bf[:], mask_cols[:],
                                              start=False, stop=True)
                mm.then_inc(st_ready, 1)

            def p_times_v(h, s, n):
                b, p = GROUPS[n]
                if n == 0:
                    pe.wait_ge(v_lo_ready, h * 4 + 4)
                if p == 0:
                    wait(pe, pv_drained, h * NB + b)
                pe.wait_ge(*lo_sem(h, n))
                for k in range(2):
                    kt = 2 * p + k
                    for j in range(max(0, kt - 4 * b), 4):
                        out = pv4[:, j // 2, j % 2, :]
                        cols = slice(k * BLK + j * P, k * BLK + (j + 1) * P)
                        nc.tensor.matmul(out, p_hi[:, n % PRING, cols], v_parts[s][:, kt, :],
                                         start=(kt == 0 and j % 2 == 0), stop=False, skip_group_check=True)
                        mm = nc.tensor.matmul(out[:, 0:D + 1], p_lo[:, n % PRING, cols], v_parts[s][:, kt, 0:D + 1],
                                              start=False, stop=(kt == 4 * b + j), skip_group_check=True)
                mm.then_inc(p_used, 1)

            pe.wait_ge(ones_ready, 1)
            layer_norm(0)
            pe.wait_ge(xn_lo_ready, NB)
            pe.wait_ge(consts, N_CONST)
            for k, task in enumerate(PROLOGUE):
                background_task(task, k, bg_bank(k), 0, 0, None)

            def body(i, first, last):
                base, at = bg_base(i, first), bg_base(0 if first else 1, first)
                for s in range(2):
                    h = i * 2 + s
                    slots = background(s, first, last)
                    for n in range(NG):
                        scores(h, s, n)
                        for task in slots[n]:
                            background_task(task, base, bg_bank(at), h + 1, 1 - s, i if s else i - 1)
                            base, at = base + 1, at + 1
                        m = (n - LAG) % NG
                        if m < n:
                            p_times_v(h, s, m)
                        elif not (first and s == 0):
                            p_times_v(h - 1, 1 - s, m)

            pairs(pe, body)
            for n in range(NG - LAG, NG):
                p_times_v(H - 1, 1, n)
            for k, task in zip((BG_TOTAL - 2, BG_TOTAL - 1), TAIL):
                background_task(task, k, bg_bank(k), None, None, PAIRS - 1)
            pe.wait_ge(bg_drained, BG_TOTAL)
            layer_norm(1)

            pe.wait_ge(xn_ready, 2 * NB)
            for t in range(NT):
                mm = nc.tensor.matmul(st[:, 0, 0, t * EXPERTS:(t + 1) * EXPERTS], xn[:, tile(t)], gate_w[:],
                                      start=True, stop=True)
            mm.then_inc(logits_ready, 1)
            pe.wait_ge(comb_ready, 1)
            for t in range(NT):
                mm = nc.tensor.transpose(mean_bank[t // 4][0:EXPERTS, tile(t % 4)], comb[:, t, :], ident[:])
            mm.then_inc(comb_t_ready, 1)

            pe.wait_ge(ln_std, 2 * NB)
            for b in range(NB):
                nc.tensor.matmul(y_bank[b], ident[:], res[:, blk(b)], start=True, stop=False, skip_group_check=True)
            pe.wait_ge(xn_lo_ready, 2 * NB)
            pe.wait_ge(comb_t_copied, NB)

            def down(Q, s, q, final):
                b, c = divmod(q, FC)
                d = slice((2 * FC + c) * P, (2 * FC + c + 1) * P)
                pe.wait_ge(h_lo_ready, Q + 1)
                mm3(y_bank[b], e_hi[s][:, d], e_lo[s][:, d], h_hi[:, q % HRING], h_lo[:, q % HRING],
                    False, final and c == FC - 1, skip=True).then_inc(down_done, 1)

            def body(p, s, first, last):
                pe.wait_ge(e_lo_ready, p + 1)
                for q in range(STEPS):
                    Q = p * STEPS + q
                    b, c = divmod(q, FC)
                    wait(pe, h_ready, Q - 1)
                    g = slice(c * P, (c + 1) * P)
                    u = slice((FC + c) * P, (FC + c + 1) * P)
                    if not first and c == 0:
                        pe.wait_ge(xw_lo_ready, (p - 1) * NB + b + 1)
                    up_hi, up_lo = (xn_hi, xn_lo) if first else (xw_hi[s], xw_lo[s])
                    mm3(st[:, q % 2, 0, :], e_hi[s][:, g], e_lo[s][:, g], xn_hi[:, blk(b)], xn_lo[:, blk(b)],
                        True, True)
                    mm3(st[:, q % 2, 1, :], e_hi[s][:, u], e_lo[s][:, u], up_hi[:, blk(b)], up_lo[:, blk(b)],
                        True, True).then_inc(gu_ready, 1)
                    m = (q - FLAG) % STEPS
                    if m < q:
                        down(Q - FLAG, s, m, last)
                    elif not first:
                        down(Q - FLAG, 1 - s, m, False)

            passes(pe, body)
            for q in range(STEPS - FLAG, STEPS):
                down(8 * STEPS + q, 1, q, True)


def kernel(L0_attn_x, L0_attn_qkv_w, L0_attn_qkv_b, L0_attn_out_w, L0_attn_out_b, L0_ffn_gate_w,
           L0_ffn_expert_gate, L0_ffn_expert_up, L0_ffn_expert_down, L0_ffn_shared_gate, L0_ffn_shared_up,
           L0_ffn_shared_down):
    import numpy as np
    import concourse.bacc as bacc
    from concourse.bass_utils import run_bass_kernel_spmd

    def rows(*parts):
        return np.concatenate([np.asarray(p) for p in parts], axis=0)

    gates = rows(L0_ffn_expert_gate, np.asarray(L0_ffn_shared_gate)[None])
    ups = rows(L0_ffn_expert_up, np.asarray(L0_ffn_shared_up)[None])
    downs = rows(L0_ffn_expert_down, np.asarray(L0_ffn_shared_down)[None])
    ffn_w = np.zeros((EXPERTS + 1, P, 3 * FC * P), np.float32)
    ffn_w[:, :, 0:F] = gates.transpose(0, 2, 1)
    ffn_w[:, :, FC * P:FC * P + F] = ups.transpose(0, 2, 1)
    down_t = np.zeros((EXPERTS + 1, FC * P, P), np.float32)
    down_t[:, 0:F, :] = downs.transpose(0, 2, 1)
    ffn_w[:, :, 2 * FC * P:] = down_t.reshape(EXPERTS + 1, FC, P, P).transpose(0, 2, 1, 3).reshape(
        EXPERTS + 1, P, FC * P)
    bias = np.asarray(L0_attn_qkv_b)
    arrays = {
        "x_t": np.asarray(L0_attn_x)[0].T,
        "qkv_w": np.asarray(L0_attn_qkv_w),
        "qk_bias_in": bias[:, 0:2 * D].reshape(H, P, 1),
        "v_bias": bias[:, 2 * D:3 * D],
        "out_w": np.asarray(L0_attn_out_w).reshape(H * D, P),
        "out_bias": np.asarray(L0_attn_out_b).reshape(P, 1),
        "gate_w_t": np.asarray(L0_ffn_gate_w).T,
        "ffn_w": ffn_w,
    }
    arrays = {n: np.ascontiguousarray(a) for n, a in arrays.items()}
    nc = bacc.Bacc("TRN2", target_bir_lowering=False, num_devices=1)
    args = [nc.dram_tensor(n, a.shape, mybir.dt.from_np(a.dtype), kind="ExternalInput").ap()
            for n, a in arrays.items()]
    args.append(nc.dram_tensor("out_t", (P, T), F32, kind="ExternalOutput").ap())
    layer_kernel(nc, *args)
    r = run_bass_kernel_spmd(nc, [arrays], core_ids=[0])
    return np.ascontiguousarray(np.asarray(r.results[0]["out_t"]).T)[None]
```

```python
from contextlib import ExitStack

import concourse.bass as bass
from concourse import mybir

F32, F32R = mybir.dt.float32, mybir.dt.float32r
F16, BF16, U32 = mybir.dt.float16, mybir.dt.bfloat16, mybir.dt.uint32
ALU, ACT = mybir.AluOpType, mybir.ActivationFunctionType
AX_X = mybir.AxisListType.X

P = 128
T = 2048
BLK = 512
NB = T // BLK
NT = T // P
H, D = 16, 64
PAIRS = H // 2
VW = 2 * D + 1
GROUPS = [(b, p) for b in range(NB) for p in range(2 * (b + 1))]
NG = len(GROUPS)
PRING, STRING, BGRING, QKRING = 5, 2, 2, 4
LAG = 3
EPS = 1e-5
NEG = -1.0e30
P_SCALE_LN = 2.772588722239781
F, FC = 352, 3
EXPERTS = 8
SHARED = EXPERTS
STEPS = NB * FC
HRING = 4
FLAG = 3

V_SLOTS = (5, 7, 9, 11)
MAX_FROM, MAX_TO, SHIFT_SLOT = 3, 18, 18
SUB_ON_DVE = (0, 2, 4, 7, 10, 14, 17)


def ends_block(n):
    b, p = GROUPS[n]
    return p == 2 * b + 1


def spread(units, tasks):
    if not units:
        return list(tasks)
    order, done = [], 0
    for k, unit in enumerate(units):
        order.append(unit)
        upto = -(-len(tasks) * (k + 1) // len(units))
        order += tasks[done:upto]
        done = upto
    return order


def sub_on_pool(n):
    return n not in SUB_ON_DVE


def vector_room(n):
    room = 1.6 if ends_block(n) else 2.6
    room -= 0.0 if sub_on_pool((n - 1) % NG) else 0.9
    room -= 0.5 if ends_block((n - LAG - 1) % NG) else 0.0
    room -= 0.3 if n in V_SLOTS else 0.0
    room -= 0.6 if n <= 4 else 0.0
    return max(room, 0.1)


def background(s, first, last):
    slots = [[] for _ in range(NG)]
    if not (last and s == 1):
        for k in range(4):
            slots[k].append(("qk", k))
            slots[V_SLOTS[k]].append(("v", k))
        chunks = [("max", t, c) for t in range(NT) for c in range((t + 4) // 4)]
        share = [vector_room(n) for n in range(MAX_FROM, MAX_TO)]
        room, n = 0.0, MAX_FROM - 1
        for task in chunks:
            while room < 0.5:
                n += 1
                room += len(chunks) * share[n - MAX_FROM] / sum(share)
            slots[n].append(task)
            room -= 1.0
        slots[SHIFT_SLOT].append(("shift",))
    if s == 0 and not first:
        slots[4].append(("att_t", 3))
        slots[7].append(("att_y", 3))
    if s == 1:
        for b, n in ((0, 6), (1, 10), (2, 16)):
            slots[n].append(("att_t", b))
            slots[n + 3].append(("att_y", b))
    return slots


def count(slots):
    return sum(map(len, slots))


PROLOGUE = sum((s for s in background(1, False, False)), [])
PROLOGUE = [t for t in PROLOGUE if not t[0].startswith("att")]
N_FIRST = count(background(0, True, False)) + count(background(1, True, False))
N_LOOP = count(background(0, False, False)) + count(background(1, False, False))
N_LAST = count(background(0, False, True)) + count(background(1, False, True))
TAIL = [("att_t", 3), ("att_y", 3)]
BG_TOTAL = len(PROLOGUE) + N_FIRST + N_LOOP * (PAIRS - 2) + N_LAST + len(TAIL)
assert N_LOOP % BGRING == 0


def bg_base(i, first):
    return len(PROLOGUE) if first else (i - 1) * N_LOOP + (len(PROLOGUE) + N_FIRST)


def bg_bank(k_static):
    return k_static % BGRING


def wait(eng, sem, value):
    if not isinstance(value, int) or value > 0:
        eng.wait_ge(sem, value)


def layer_kernel(nc, x_t, qkv_w, qk_bias_in, v_bias, out_w, out_bias, gate_w_t, ffn_w, out_t):
    ctx = ExitStack()
    with ctx:
        def sb(name, shape, dtype):
            return ctx.enter_context(nc.sbuf_tensor(name, shape, dtype))

        def psum(name, shape, dtype):
            return ctx.enter_context(nc.psum_tensor(name, shape, dtype))

        def sem(name):
            return ctx.enter_context(nc.semaphore(name))

        res = sb("res", [P, T], F32)
        xn = sb("xn", [P, T], F32)
        xn_hi = sb("xn_hi", [P, T], F32R)
        xn_lo = sb("xn_lo", [P, T], F32R)
        q_hihi = [sb(f"q_hihi{s}", [P, T], F32R) for s in range(2)]
        k_lohi = [sb(f"k_lohi{s}", [P, T], F32R) for s in range(2)]
        q_lo_shift = [sb(f"q_lo_shift{s}", [P, T], F32R) for s in range(2)]
        k_hi_one = [sb(f"k_hi_one{s}", [P, T], F32R) for s in range(2)]
        v_parts = [sb(f"v_parts{s}", [P, NT, VW], F16) for s in range(2)]
        v32 = sb("v32", [P, 2, 4, D], F32)
        prob = sb("prob", [P, PRING, 2 * BLK], F32)
        p_hi = sb("p_hi", [P, PRING, 2 * BLK], F16)
        p_lo = sb("p_lo", [P, PRING, 2 * BLK], F16)
        row_max = sb("row_max", [P, NT, NB], F32)
        neg_max = sb("neg_max", [P, NT], F32)
        shift_row = sb("shift_row", [NT, P], F32R)
        std = sb("std", [P, NT], F32)
        rstd = sb("rstd", [P, NT], F32)
        attn = sb("attn", [P, NT, 2 * D], F32)
        qk32 = sb("qk32", [P, QKRING, BLK], F32)
        pv32 = sb("pv32", [P, 4, VW], F32)
        pv_sum = sb("pv_sum", [P, 4, D], F32)
        att32 = sb("att32", [P, BLK], F32)
        rden = sb("rden", [P, 4, 1], F32)
        att_hi = sb("att_hi", [P, BLK], F32R)
        att_lo = sb("att_lo", [P, BLK], F32R)
        w_raw = [sb(f"w_raw{s}", [P, 3 * D], F32) for s in range(2)]
        w_hi = [sb(f"w_hi{s}", [P, 2 * D], F32R) for s in range(2)]
        w_lo = [sb(f"w_lo{s}", [P, 2 * D], F32R) for s in range(2)]
        qk_bias = [sb(f"qk_bias{s}", [P, 1], F32) for s in range(2)]
        vb = [sb(f"vb{s}", [P, D], F32) for s in range(2)]
        wo_raw = sb("wo_raw", [P, P], F32)
        wo_hi = sb("wo_hi", [P, P], F32R)
        wo_lo = sb("wo_lo", [P, P], F32R)
        obias = sb("obias", [P, 1], F32)
        ones_mean = sb("ones_mean", [P, P], F32)
        ident = sb("ident", [P, P], F32)
        ident_bf = sb("ident_bf", [P, P], BF16)
        mask_rows = sb("mask_rows", [P, P], BF16)
        mask_cols = sb("mask_cols", [P, P], BF16)
        eps = sb("eps", [P, 1], F32)
        p_bias = sb("p_bias", [P, 1], F32)
        gate_w = sb("gate_w", [P, EXPERTS], F32)
        lg = sb("lg", [P, NT, EXPERTS], F32)
        lg_max = sb("lg_max", [P, NT, 1], F32)
        pr = sb("pr", [P, NT, EXPERTS], F32)
        pr_sum = sb("pr_sum", [P, NT, 1], F32)
        top = sb("top", [P, NT, 8], F32)
        top_at = sb("top_at", [P, NT, 8], U32)
        top_atf = sb("top_atf", [P, NT, 2], F32)
        top_w = sb("top_w", [P, NT, 2], F32)
        wsum = sb("wsum", [P, NT, 1], F32)
        iota8 = sb("iota8", [P, 1, EXPERTS], F32)
        hot = sb("hot", [P, 2, NT, EXPERTS], F32)
        comb = sb("comb", [P, NT, EXPERTS], F32)
        xw32 = sb("xw32", [P, 2, BLK], F32)
        e_raw = [sb(f"e_raw{s}", [P, 3 * FC * P], F32) for s in range(2)]
        h_lo = sb("h_lo", [P, HRING, BLK], F32R)
        sq = prob[:, 0:2, :].rearrange("p a b -> p (a b)")
        pflat = prob[:, :, :].rearrange("p a b -> p (a b)")
        silu = [pflat[:, k * BLK:(k + 1) * BLK] for k in range(HRING)]
        h32 = [pflat[:, (HRING + k) * BLK:(HRING + k + 1) * BLK] for k in range(HRING)]
        e_hi, e_lo = k_hi_one, q_lo_shift
        h_hi = [t[:, 3 * FC * P:3 * FC * P + BLK] for t in e_hi + e_lo]
        xw_hi, xw_lo = q_hihi, k_lohi
        w_tok = attn[:, :, :].rearrange("p a b -> p (a b)")
        comb_t = w_tok[0:EXPERTS, :]
        comb_dram = nc.dram_tensor("comb_dram", [EXPERTS, T], F32, kind="Internal").ap()

        st = psum("st", [P, STRING, 2, BLK], F32)
        bg = psum("bg", [P, BGRING, BLK], F32)
        pv = psum("pv", [P, 2, BLK], F32)
        pv4 = pv[:, :, 0:2 * VW].rearrange("p a (j c) -> p a j c", c=VW)
        mean_bank = [st[:, b // 2, b % 2, :] for b in range(NB)]
        y_bank = [bg[:, 0, :], bg[:, 1, :], pv[:, 0, :], pv[:, 1, :]]

        x_landed = [sem(f"x_landed{b}") for b in range(NB)]
        small_landed = sem("small_landed")
        head_w_landed = [sem(f"head_w_landed{s}") for s in range(2)]
        wo_landed, wo_hi_ready, wo_lo_ready = sem("wo_landed"), sem("wo_hi_ready"), sem("wo_lo_ready")
        w_hi_ready, w_lo_ready = sem("w_hi_ready"), sem("w_lo_ready")
        consts, pool_self = sem("consts"), sem("pool_self")
        one_rows = sem("one_rows")
        ones_ready, eps_ready = sem("ones_ready"), sem("eps_ready")
        ln_mean, ln_centered, ln_sq, ln_var = sem("ln_mean"), sem("ln_centered"), sem("ln_sq"), sem("ln_var")
        ln_std, ln_rstd, ln_spread, xn_ready = sem("ln_std"), sem("ln_rstd"), sem("ln_spread"), sem("xn_ready")
        xn_hi_ready, xn_lo_ready = sem("xn_hi_ready"), sem("xn_lo_ready")
        res_ready = sem("res_ready")
        st_ready, exp_done = sem("st_ready"), sem("exp_done")
        lo_dve, lo_pool = sem("lo_dve"), sem("lo_pool")
        p_used, rden_ready, pv_drained, attn_ready = sem("p_used"), sem("rden_ready"), sem("pv_drained"), sem("attn_ready")
        evac_self = sem("evac_self")
        bg_ready, bg_drained = sem("bg_ready"), sem("bg_drained")
        qk_hi_ready, k_dup_landed = sem("qk_hi_ready"), sem("k_dup_landed")
        q_dup_landed = [sem(f"q_dup_landed{b}") for b in range(NB)]
        q_lo_ready, k_lo_ready = sem("q_lo_ready"), sem("k_lo_ready")
        v_hi_ready, v_lo_ready = sem("v_hi_ready"), sem("v_lo_ready")
        neg_max_ready, shift_landed = sem("neg_max_ready"), sem("shift_landed")
        att_hi_ready, att_lo_ready = sem("att_hi_ready"), sem("att_lo_ready")
        logits_ready, router_max, router, router_exp, comb_ready = sem("logits_ready"), sem("router_max"), sem("router"), sem("router_exp"), sem("comb_ready")
        comb_t_ready, comb_t_copied, comb_stored = sem("comb_t_ready"), sem("comb_t_copied"), sem("comb_stored")
        e_landed = [sem(f"e_landed{s}") for s in range(2)]
        w_tok_landed, xw_ready, xw_hi_ready, xw_lo_ready = sem("w_tok_landed"), sem("xw_ready"), sem("xw_hi_ready"), sem("xw_lo_ready")
        e_hi_ready, e_lo_ready = sem("e_hi_ready"), sem("e_lo_ready")
        gu_ready, silu_done, h_ready = sem("gu_ready"), sem("silu_done"), sem("h_ready")
        h_hi_ready, h_lo_ready, down_done = sem("h_hi_ready"), sem("h_lo_ready"), sem("down_done")
        out_copied_act, out_copied_dve, out_stored = sem("out_copied_act"), sem("out_copied_dve"), sem("out_stored")

        N_CONST = 8
        pool_per_head = sum(sub_on_pool(n) for n in range(NG))
        dve_per_head = NG - pool_per_head

        def lo_sem(G_head, n):
            if sub_on_pool(n):
                return lo_pool, G_head * pool_per_head + sum(sub_on_pool(k) for k in range(n + 1))
            return lo_dve, G_head * dve_per_head + sum(not sub_on_pool(k) for k in range(n + 1))

        def columns(n):
            b, p = GROUPS[n]
            return (256 if p == 2 * b + 1 else 0), BLK

        def blk(b):
            return slice(b * BLK, (b + 1) * BLK)

        def tile(t):
            return slice(t * P, (t + 1) * P)

        def max_width(t, c):
            return min(BLK, P * (t + 1) - BLK * c)

        def v_quad(slot, q, lo, hi):
            return v_parts[slot][:, 4 * q:4 * q + 4, lo:hi]

        def pairs(eng, body):
            body(0, True, False)
            with eng.Fori(1, PAIRS - 1) as i:
                body(i, False, False)
            body(PAIRS - 1, False, True)

        def passes(eng, body):
            body(0, 1, True, False)
            with eng.Fori(0, 3) as j:
                body(j * 2 + 1, 0, False, False)
                body(j * 2 + 2, 1, False, False)
            body(7, 0, False, False)
            body(8, 1, False, True)

        block = ctx.enter_context(nc.Block())

        @block.sync
        def _(sp):
            def head_weights(h, s):
                hs = bass.ds(h, 1)
                sp.dma_start(w_raw[s][:], qkv_w[:, hs, :].rearrange("e h d -> e (h d)")).then_inc(head_w_landed[s], 16)
                sp.dma_start(qk_bias[s][:], qk_bias_in[hs, :, :].rearrange("o p c -> (o p) c")).then_inc(head_w_landed[s], 16)
                sp.dma_start(vb[s][:], v_bias[hs, :].broadcast_to([P, D])).then_inc(head_w_landed[s], 16)

            for b in range(NB):
                sp.dma_start(res[:, blk(b)], x_t[:, blk(b)]).then_inc(x_landed[b], 16)
            head_weights(0, 0)
            sp.dma_start(obias[:], out_bias).then_inc(small_landed, 16)
            sp.dma_start(gate_w[:], gate_w_t).then_inc(small_landed, 16)

            def dup_and_shift(h, s, shift_count):
                for b in range(NB):
                    sp.wait_ge(qk_hi_ready, h * NB + b + 1)
                    sp.dma_start(q_hihi[s][D:P, blk(b)].bitcast(F32), q_hihi[s][0:D, blk(b)].bitcast(F32)
                                 ).then_inc(q_dup_landed[b], 16)
                sp.dma_start(k_hi_one[s][0:D, :].bitcast(F32), k_lohi[s][D:P, :].bitcast(F32)).then_inc(k_dup_landed, 16)
                sp.wait_ge(bg_drained, shift_count)
                sp.dma_start(q_lo_shift[s][D:D + 1, :].bitcast(F32),
                             shift_row[:, :].bitcast(F32)).then_inc(shift_landed, 16)

            head_weights(1, 1)
            dup_and_shift(0, 0, len(PROLOGUE))

            def body(i, first, last):
                base = bg_base(i, first)
                for s in range(2):
                    h = i * 2 + s
                    tasks = sum(background(s, first, last), [])
                    sp.wait_ge(st_ready, h * NG + 1)
                    if s == 0:
                        wait(sp, wo_lo_ready, i)
                        sp.dma_start(wo_raw[:], out_w[bass.ds(i * P, P), :]).then_inc(wo_landed, 16)
                    if not last:
                        head_weights(h + 2, s)
                    if not (last and s == 1):
                        dup_and_shift(h + 1, 1 - s, base + tasks.index(("shift",)) + 1)
                    base = base + len(tasks)

            pairs(sp, body)

            def expert_weights(p, s, expert):
                sp.dma_start(e_raw[s][:], ffn_w[bass.ds(expert, 1), :, :].rearrange("o p w -> (o p) w")
                             ).then_inc(e_landed[s], 16)

            expert_weights(0, 1, SHARED)
            expert_weights(1, 0, 0)
            sp.wait_ge(comb_t_copied, 4)
            sp.dma_start(comb_dram, comb_t).then_inc(comb_stored, 16)
            sp.wait_ge(comb_stored, 16)

            def body(p, s, first, last):
                if last:
                    return
                if not first:
                    sp.wait_ge(xw_ready, p * NB)
                sp.dma_start(w_tok[:], comb_dram[bass.ds(p, 1), :].broadcast_to([P, T])
                             ).then_inc(w_tok_landed, 16)
                if isinstance(p, int) and p >= 7:
                    return
                sp.wait_ge(e_hi_ready, p + 1)
                sp.wait_ge(e_lo_ready, p + 1)
                expert_weights(p + 2, s, p + 1)

            passes(sp, body)
            for b in range(NB):
                done = (out_copied_act, out_copied_dve)[b % 2]
                sp.wait_ge(done, b // 2 + 1)
                sp.dma_start(out_t[:, blk(b)], xn[:, blk(b)]).then_inc(out_stored, 16)
            sp.wait_ge(out_stored, 16 * NB)

        @block.gpsimd
        def _(pool):
            nc.gpsimd.memset(ones_mean[:], 1.0 / P).then_inc(ones_ready, 1)
            nc.gpsimd.memset(ident[:], 0.0).then_inc(pool_self, 1)
            pool.wait_ge(pool_self, 1)
            nc.gpsimd.affine_select(out=ident[:], in_=ident[:], compare_op=ALU.not_equal, fill=1.0, base=0,
                                    pattern=[[-1, P]], channel_multiplier=1).then_inc(ones_ready, 1)
            nc.gpsimd.memset(eps[:], EPS).then_inc(eps_ready, 1)
            nc.gpsimd.memset(p_bias[:], P_SCALE_LN).then_inc(consts, 1)
            nc.gpsimd.memset(ident_bf[:], 0.0).then_inc(pool_self, 1)
            nc.gpsimd.memset(mask_rows[:], 0.0).then_inc(pool_self, 1)
            nc.gpsimd.memset(mask_cols[:], 0.0).then_inc(pool_self, 1)
            pool.wait_ge(pool_self, 4)
            nc.gpsimd.affine_select(out=ident_bf[:], in_=ident_bf[:], compare_op=ALU.not_equal, fill=1.0, base=0,
                                    pattern=[[-1, P]], channel_multiplier=1).then_inc(consts, 1)
            nc.gpsimd.affine_select(out=mask_rows[:], in_=mask_rows[:], compare_op=ALU.is_ge, fill=NEG, base=0,
                                    pattern=[[-1, P]], channel_multiplier=1).then_inc(consts, 1)
            nc.gpsimd.affine_select(out=mask_cols[:], in_=mask_cols[:], compare_op=ALU.is_ge, fill=NEG, base=0,
                                    pattern=[[1, P]], channel_multiplier=-1).then_inc(consts, 1)
            for s in range(2):
                nc.gpsimd.memset(v_parts[s][:, :, D:D + 1], 1.0).then_inc(consts, 1)
            nc.gpsimd.memset(row_max[:], -3.0e38).then_inc(consts, 1)
            nc.gpsimd.iota(iota8[:, 0, :], pattern=[[1, EXPERTS]], base=0, channel_multiplier=0,
                           allow_small_or_imprecise_dtypes=True).then_inc(consts, 1)
            pool.wait_ge(small_landed, 32)
            pool.wait_ge(ln_centered, NB)
            nc.gpsimd.tensor_scalar(res[:], res[:], obias[:, 0:1], None, ALU.add).then_inc(res_ready, 1)

            def v_low(h, s, q):
                pool.wait_ge(v_hi_ready, h * 4 + q + 1)
                nc.gpsimd.tensor_tensor(v_quad(s, q, D + 1, VW), v32[:, q % 2], v_quad(s, q, 0, D),
                                        ALU.subtract).then_inc(v_lo_ready, 1)

            def background_task(task, k, h, s, pair):
                if task[0] == "qk":
                    b = task[1]
                    pool.wait_ge(qk_hi_ready, h * NB + b + 1)
                    nc.gpsimd.tensor_tensor(q_lo_shift[s][0:D, blk(b)], qk32[0:D, b % QKRING], q_hihi[s][0:D, blk(b)],
                                            ALU.subtract).then_inc(q_lo_ready, 1)
                elif task[0] == "v":
                    v_low(h, s, task[1])
                elif task[0] == "att_t":
                    pool.wait_ge(att_hi_ready, pair * NB + task[1] + 1)
                    nc.gpsimd.tensor_tensor(att_lo[:], att32[:], att_hi[:], ALU.subtract).then_inc(att_lo_ready, 1)

            for task in PROLOGUE:
                background_task(task, None, 0, 0, None)

            def p_low(h, n):
                G = h * NG + n
                lo, hi = columns(n)
                pool.wait_ge(exp_done, G + 1)
                ring = n % PRING
                a = prob[:, ring].rearrange("p (k c) -> p k c", k=2)[:, :, lo:hi]
                b = p_hi[:, ring].rearrange("p (k c) -> p k c", k=2)[:, :, lo:hi]
                o = p_lo[:, ring].rearrange("p (k c) -> p k c", k=2)[:, :, lo:hi]
                nc.gpsimd.tensor_tensor(o, a, b, ALU.subtract).then_inc(lo_pool, 1)

            def normalise(h, s, n):
                b = GROUPS[n][0]
                B = h * NB + b
                pool.wait_ge(rden_ready, B + 1)
                nc.gpsimd.tensor_tensor(pv_sum[:], pv32[:, :, 0:D], pv32[:, :, D + 1:VW], ALU.add
                                        ).then_inc(evac_self, 1)
                pool.wait_ge(evac_self, B + 1)
                nc.gpsimd.tensor_tensor(attn[:, 4 * b:4 * b + 4, s * D:(s + 1) * D], pv_sum[:],
                                        rden[:].broadcast_to([P, 4, D]), ALU.mult).then_inc(attn_ready, 1)

            def body(i, first, last):
                for s in range(2):
                    h = i * 2 + s
                    slots = background(s, first, last)
                    for n in range(NG):
                        m = (n - LAG - 1) % NG
                        if ends_block(m) and not (first and s == 0 and m > n):
                            normalise(h if m < n else h - 1, s if m < n else 1 - s, m)
                        for task in slots[n]:
                            if task[0] == "v":
                                background_task(task, None, h + 1, 1 - s, i if s else i - 1)
                        if sub_on_pool(n):
                            p_low(h, n)
                        for task in slots[n - 1] if n else []:
                            if task[0] in ("att_t", "qk"):
                                background_task(task, None, h + 1, 1 - s, i if s else i - 1)

            pairs(pool, body)
            normalise(H - 1, 1, NG - 1)

            def expert_lo(p, s):
                pool.wait_ge(e_hi_ready, p + 1)
                nc.gpsimd.tensor_tensor(e_lo[s][:, 0:3 * FC * P], e_raw[s][:], e_hi[s][:, 0:3 * FC * P],
                                        ALU.subtract).then_inc(e_lo_ready, 1)

            def weighted_input(p, b):
                if b == 0:
                    pool.wait_ge(w_tok_landed, p * 16 + 16)
                wait(pool, xw_lo_ready, p * NB + b - 1)
                nc.gpsimd.tensor_tensor(xw32[:, b % 2], xn[:, blk(b)], w_tok[:, blk(b)], ALU.mult
                                        ).then_inc(xw_ready, 1)

            def weighted_lo(p, s, b):
                pool.wait_ge(xw_hi_ready, p * NB + b + 1)
                nc.gpsimd.tensor_tensor(xw_lo[s][:, blk(b)], xw32[:, b % 2], xw_hi[s][:, blk(b)], ALU.subtract
                                        ).then_inc(xw_lo_ready, 1)

            expert_lo(0, 1)
            background_task(TAIL[0], None, None, None, PAIRS - 1)
            pool.wait_ge(xn_ready, 2 * NB)

            def body(p, s, first, last):
                if last:
                    return
                weighted_input(p, 0)
                weighted_input(p, 1)
                expert_lo(p + 1, 1 - s)
                for b in range(NB):
                    weighted_lo(p, 1 - s, b)
                    if b + 2 < NB:
                        weighted_input(p, b + 2)

            passes(pool, body)

        @block.scalar
        def _(act):
            def deviation(turn, b):
                act.wait_ge(ln_var, turn * NB + b + 1)
                nc.scalar.activation(std[:, 4 * b:4 * b + 4], y_bank[b][:, 0:4], ACT.Sqrt, bias=eps[:]
                                     ).then_inc(ln_std, 1)

            def layer_norm(turn):
                for b in range(NB):
                    act.wait_ge(ln_centered, turn * NB + b + 1)
                    nc.scalar.activation(sq[:, blk(b)], xn[:, blk(b)], ACT.Square).then_inc(ln_sq, 1)
                    if b:
                        deviation(turn, b - 1)
                deviation(turn, NB - 1)
                for b in range(NB):
                    act.wait_ge(xn_ready, turn * NB + b + 1)
                    nc.scalar.copy(xn_hi[:, blk(b)], xn[:, blk(b)]).then_inc(xn_hi_ready, 1)

            def split_head_weights(h, s, landed):
                act.wait_ge(head_w_landed[s], landed)
                nc.scalar.copy(w_hi[s][:], w_raw[s][:, 0:2 * D]).then_inc(w_hi_ready, 1)

            def background_task(task, k, bank, h, s):
                if task[0] == "qk":
                    b = task[1]
                    act.wait_ge(bg_drained, k + 1)
                    nc.scalar.copy(q_hihi[s][0:D, blk(b)], qk32[0:D, b % QKRING])
                    nc.scalar.copy(k_lohi[s][D:P, blk(b)], qk32[D:P, b % QKRING]).then_inc(qk_hi_ready, 1)
                elif task[0] == "v":
                    q = task[1]
                    act.wait_ge(bg_drained, k + 1)
                    nc.scalar.copy(v_quad(s, q, 0, D), v32[:, q % 2]).then_inc(v_hi_ready, 1)
                elif task[0] == "att_t":
                    act.wait_ge(bg_drained, k + 1)
                    nc.scalar.copy(att_hi[:], att32[:]).then_inc(att_hi_ready, 1)

            def exps(h, n):
                G = h * NG + n
                lo, hi = columns(n)
                act.wait_ge(st_ready, G + 1)
                wait(act, p_used, G - PRING + 1)
                src = st[:, n % STRING, :, lo:hi]
                o32 = prob[:, n % PRING].rearrange("p (k c) -> p k c", k=2)[:, :, lo:hi]
                o16 = p_hi[:, n % PRING].rearrange("p (k c) -> p k c", k=2)[:, :, lo:hi]
                nc.scalar.activation(o32, src, ACT.Exp, bias=p_bias[:], scale=D ** -0.5)
                nc.scalar.activation(o16, src, ACT.Exp, bias=p_bias[:], scale=D ** -0.5).then_inc(exp_done, 1)

            split_head_weights(0, 0, 48)
            act.wait_ge(eps_ready, 1)
            layer_norm(0)
            act.wait_ge(consts, N_CONST)
            for k, task in enumerate(PROLOGUE):
                background_task(task, k, bg_bank(k), 0, 0)
            split_head_weights(1, 1, 48)

            def body(i, first, last):
                base, at = bg_base(i, first), bg_base(0 if first else 1, first)
                late = None
                for s in range(2):
                    h = i * 2 + s
                    slots = background(s, first, last)
                    for n in range(NG):
                        exps(h, n)
                        for task in slots[n]:
                            if task[0] == "att_t":
                                late = (task, base, bg_bank(at), h + 1, 1 - s)
                            else:
                                background_task(task, base, bg_bank(at), h + 1, 1 - s)
                            base, at = base + 1, at + 1
                        if late and not any(t[0] == "att_t" for t in slots[n]):
                            background_task(*late)
                            late = None
                        if n == 10 and not last:
                            split_head_weights(h + 2, s, (i + 2) * 48)
                        if n == 10 and s == 0:
                            act.wait_ge(wo_landed, i * 16 + 16)
                            wait(act, bg_drained, base)
                            nc.scalar.copy(wo_hi[:], wo_raw[:]).then_inc(wo_hi_ready, 1)

            pairs(act, body)

            def expert_hi(p, s, landed):
                act.wait_ge(e_landed[s], landed)
                nc.scalar.copy(e_hi[s][:, 0:3 * FC * P], e_raw[s][:]).then_inc(e_hi_ready, 1)

            expert_hi(0, 1, 16)
            k = BG_TOTAL - 2
            background_task(TAIL[0], k, bg_bank(k), None, None)
            layer_norm(1)

            act.wait_ge(router, 1)
            nc.scalar.activation(pr[:], lg[:], ACT.Exp).then_inc(router_exp, 1)
            for b in range(NB):
                act.wait_ge(comb_t_ready, 1)
                nc.scalar.copy(comb_t[:, blk(b)], mean_bank[b][0:EXPERTS, :]).then_inc(comb_t_copied, 1)

            def hidden_hi(Q, q):
                act.wait_ge(h_ready, Q + 1)
                wait(act, down_done, Q - HRING + 1)
                nc.scalar.copy(h_hi[q % HRING], h32[q % HRING]).then_inc(h_hi_ready, 1)

            def body(p, s, first, last):
                for q in range(STEPS):
                    Q = p * STEPS + q
                    act.wait_ge(gu_ready, Q + 1)
                    nc.scalar.activation(silu[q % HRING], st[:, q % 2, 0, :], ACT.Silu).then_inc(silu_done, 1)
                    if not (first and q == 0):
                        hidden_hi(Q - 1, (q - 1) % STEPS)
                    if last:
                        continue
                    if q == 2:
                        wait(act, down_done, p * STEPS)
                        expert_hi(p + 1, 1 - s, e_count(p, s))
                    if 3 <= q < 3 + NB:
                        b = q - 3
                        act.wait_ge(xw_ready, p * NB + b + 1)
                        nc.scalar.copy(xw_hi[1 - s][:, blk(b)], xw32[:, b % 2]).then_inc(xw_hi_ready, 1)

            def e_count(p, s):
                return (p + 1) * 8 + 16 if s == 0 else (p + 2) * 8

            passes(act, body)
            hidden_hi(9 * STEPS - 1, STEPS - 1)
            for b in (0, 2):
                act.wait_ge(down_done, 8 * STEPS + FC * (b + 1))
                nc.scalar.copy(xn[:, blk(b)], y_bank[b]).then_inc(out_copied_act, 1)

        @block.vector
        def _(dve):
            def normal(turn, b):
                dve.wait_ge(ln_spread, turn * NB + b + 1)
                nc.vector.tensor_tensor(xn[:, blk(b)], xn[:, blk(b)], mean_bank[b], ALU.mult).then_inc(xn_ready, 1)
                if b:
                    low_part(turn, b - 1)

            def low_part(turn, b):
                dve.wait_ge(xn_hi_ready, turn * NB + b + 1)
                nc.vector.tensor_tensor(xn_lo[:, blk(b)], xn[:, blk(b)], xn_hi[:, blk(b)], ALU.subtract
                                        ).then_inc(xn_lo_ready, 1)

            def layer_norm(turn):
                for b in range(NB):
                    if turn == 0:
                        dve.wait_ge(x_landed[b], 16)
                    dve.wait_ge(ln_mean, turn * NB + b + 1)
                    nc.vector.tensor_tensor(xn[:, blk(b)], res[:, blk(b)], mean_bank[b], ALU.subtract
                                            ).then_inc(ln_centered, 1)
                for b in range(NB):
                    dve.wait_ge(ln_std, turn * NB + b + 1)
                    nc.vector.reciprocal(rstd[:, 4 * b:4 * b + 4], std[:, 4 * b:4 * b + 4]).then_inc(ln_rstd, 1)
                    if b:
                        normal(turn, b - 1)
                normal(turn, NB - 1)
                low_part(turn, NB - 1)

            def split_head_weights(h, s):
                dve.wait_ge(w_hi_ready, h + 1)
                nc.vector.tensor_tensor(w_lo[s][:], w_raw[s][:, 0:2 * D], w_hi[s][:], ALU.subtract
                                        ).then_inc(w_lo_ready, 1)

            def background_task(task, k, bank, h, s, maxes, att):
                dve.wait_ge(bg_ready, k + 1)
                if task[0] == "qk":
                    b = task[1]
                    wait(dve, q_lo_ready, h * NB + b - QKRING + 1)
                    wait(dve, k_lo_ready, h * NB + b - QKRING + 1)
                    nc.vector.tensor_scalar(qk32[:, b % QKRING], bg[:, bank], qk_bias[s][:, 0:1], None, ALU.add
                                            ).then_inc(bg_drained, 1)
                elif task[0] == "v":
                    q = task[1]
                    wait(dve, v_lo_ready, h * 4 + q - 1)
                    nc.vector.tensor_tensor(v32[:, q % 2], bg[:, bank].rearrange("p (r c) -> p r c", r=4)[:, :, D:P],
                                            vb[s][:].unsqueeze(1).broadcast_to([P, 4, D]), ALU.add
                                            ).then_inc(bg_drained, 1)
                elif task[0] == "max":
                    t, c = task[1:]
                    nc.vector.tensor_reduce(row_max[:, t, c:c + 1], bg[:, bank, 0:max_width(t, c)], AX_X,
                                            ALU.max).then_inc(bg_drained, 1)
                    if (t, c) == (NT - 1, NB - 1):
                        dve.wait_ge(bg_drained, k + 1)
                        nc.vector.tensor_reduce(neg_max[:], row_max[:], AX_X, ALU.max, negate=True
                                                ).then_inc(neg_max_ready, 1)
                elif task[0] == "shift":
                    wait(dve, shift_landed, h * 16)
                    nc.vector.tensor_copy(shift_row[:], bg[0:NT, bank, 0:P]).then_inc(bg_drained, 1)
                elif task[0] == "att_t":
                    wait(dve, att_lo_ready, att * NB + task[1])
                    nc.vector.tensor_copy(att32[:], bg[:, bank]).then_inc(bg_drained, 1)
                elif task[0] == "att_y":
                    b = task[1]
                    nc.vector.tensor_tensor(res[:, blk(b)], res[:, blk(b)], bg[:, bank], ALU.add
                                            ).then_inc(bg_drained, 1)

            def p_low(h, n, k):
                lo, hi = columns(n)
                if k == 0:
                    dve.wait_ge(exp_done, h * NG + n + 1)
                cols = slice(k * BLK + lo, k * BLK + hi)
                ring = n % PRING
                low = nc.vector.tensor_tensor(p_lo[:, ring, cols], prob[:, ring, cols], p_hi[:, ring, cols],
                                              ALU.subtract)
                if k == 1:
                    low.then_inc(lo_dve, 1)

            def key_low(h, s, b):
                dve.wait_ge(qk_hi_ready, h * NB + b + 1)
                nc.vector.tensor_tensor(k_lohi[s][0:D, blk(b)], qk32[D:P, b % QKRING], k_lohi[s][D:P, blk(b)],
                                        ALU.subtract).then_inc(k_lo_ready, 1)

            def evacuate(h, n, s):
                b = GROUPS[n][0]
                B = h * NB + b
                wait(dve, attn_ready, B)
                dve.wait_ge(p_used, h * NG + n + 1)
                nc.vector.tensor_copy(pv32[:].rearrange("p (a j) c -> p a j c", a=2), pv4).then_inc(pv_drained, 1)
                dve.wait_ge(pv_drained, B + 1)
                nc.vector.reciprocal(rden[:], pv32[:, :, D:D + 1]).then_inc(rden_ready, 1)

            nc.vector.memset(k_hi_one[0][D:D + 1, :].bitcast(F32), 1.0).then_inc(one_rows, 1)
            layer_norm(0)
            split_head_weights(0, 0)
            dve.wait_ge(consts, N_CONST)
            for k, task in enumerate(PROLOGUE):
                background_task(task, k, bg_bank(k), 0, 0, None, None)
                if k and PROLOGUE[k - 1][0] == "qk":
                    key_low(0, 0, PROLOGUE[k - 1][1])
            nc.vector.memset(k_hi_one[1][D:D + 1, :].bitcast(F32), 1.0).then_inc(one_rows, 1)
            split_head_weights(1, 1)
            dve.wait_ge(res_ready, 1)

            def body(i, first, last):
                base, at = bg_base(i, first), bg_base(0 if first else 1, first)
                for s in range(2):
                    h = i * 2 + s
                    slots = background(s, first, last)
                    for n in range(NG):
                        m = (n - LAG - 1) % NG
                        if ends_block(m) and not (first and s == 0 and m > n):
                            evacuate(h if m < n else h - 1, m, s if m < n else 1 - s)
                        m = (n - 1) % NG
                        units = []
                        if not sub_on_pool(m) and not (first and s == 0 and n == 0):
                            units = [(p_low, h if n else h - 1, m, k) for k in range(2)]
                        for item in spread(units, slots[n]):
                            if callable(item[0]):
                                item[0](*item[1:])
                                continue
                            background_task(item, base, bg_bank(at), h + 1, 1 - s, None, i if s else i - 1)
                            base, at = base + 1, at + 1
                        for task in slots[n - 1] if n else []:
                            if task[0] == "qk":
                                key_low(h + 1, 1 - s, task[1])
                        if n == 10 and not last:
                            split_head_weights(h + 2, s)
                        if n == 10 and s == 0:
                            dve.wait_ge(wo_hi_ready, i + 1)
                            nc.vector.tensor_tensor(wo_lo[:], wo_raw[:], wo_hi[:], ALU.subtract
                                                    ).then_inc(wo_lo_ready, 1)

            pairs(dve, body)
            for k in range(0 if sub_on_pool(NG - 1) else 2):
                p_low(H - 1, NG - 1, k)
            evacuate(H - 1, NG - 1, 1)
            for k, task in zip((BG_TOTAL - 2, BG_TOTAL - 1), TAIL):
                background_task(task, k, bg_bank(k), None, None, None, PAIRS - 1)
            layer_norm(1)

            steps = [0]

            def own(ins):
                steps[0] += 1
                ins.then_inc(router, 1)
                dve.wait_ge(router, steps[0])

            dve.wait_ge(logits_ready, 1)
            logits = st[:, 0, 0, 0:NT * EXPERTS].rearrange("p (t e) -> p t e", e=EXPERTS)
            nc.vector.tensor_reduce(lg_max[:, :, 0], logits, AX_X, ALU.max).then_inc(router_max, 1)
            dve.wait_ge(router_max, 1)
            own(nc.vector.tensor_tensor(lg[:], logits, lg_max[:].broadcast_to([P, NT, EXPERTS]), ALU.subtract))
            dve.wait_ge(router_exp, 1)
            own(nc.vector.tensor_reduce(pr_sum[:, :, 0], pr[:], AX_X, ALU.add))
            own(nc.vector.reciprocal(pr_sum[:], pr_sum[:]))
            own(nc.vector.tensor_tensor(pr[:], pr[:], pr_sum[:].broadcast_to([P, NT, EXPERTS]), ALU.mult))
            for t in range(NT):
                last_max = nc.vector.max(top[:, t, :], pr[:, t, :])
            own(last_max)
            for t in range(NT):
                last_at = nc.vector.max_index(top_at[:, t, :], top[:, t, :], pr[:, t, :])
            own(last_at)
            own(nc.vector.tensor_copy(top_atf[:], top_at[:, :, 0:2]))
            own(nc.vector.scalar_tensor_tensor(out=wsum[:, :, 0], in0=top[:, :, 0], scalar=1e-20, in1=top[:, :, 1],
                                               op0=ALU.add, op1=ALU.add))
            own(nc.vector.reciprocal(wsum[:], wsum[:]))
            own(nc.vector.tensor_tensor(top_w[:], top[:, :, 0:2], wsum[:].broadcast_to([P, NT, 2]), ALU.mult))
            for r in range(2):
                own(nc.vector.tensor_tensor(hot[:, r], iota8[:].broadcast_to([P, NT, EXPERTS]),
                                            top_atf[:, :, r:r + 1].broadcast_to([P, NT, EXPERTS]), ALU.is_equal))
                own(nc.vector.tensor_tensor(hot[:, r], hot[:, r],
                                            top_w[:, :, r:r + 1].broadcast_to([P, NT, EXPERTS]), ALU.mult))
            nc.vector.tensor_tensor(comb[:], hot[:, 0], hot[:, 1], ALU.add).then_inc(comb_ready, 1)

            def hidden_lo(Q, q):
                dve.wait_ge(h_hi_ready, Q + 1)
                nc.vector.tensor_tensor(h_lo[:, q % HRING], h32[q % HRING], h_hi[q % HRING],
                                        ALU.subtract).then_inc(h_lo_ready, 1)

            def body(p, s, first, last):
                for q in range(STEPS):
                    Q = p * STEPS + q
                    dve.wait_ge(silu_done, Q + 1)
                    nc.vector.tensor_tensor(h32[q % HRING], silu[q % HRING], st[:, q % 2, 1, :], ALU.mult
                                            ).then_inc(h_ready, 1)
                    if not (first and q == 0):
                        hidden_lo(Q - 1, (q - 1) % STEPS)

            passes(dve, body)
            hidden_lo(9 * STEPS - 1, STEPS - 1)
            for b in (1, 3):
                dve.wait_ge(down_done, 8 * STEPS + FC * (b + 1))
                nc.vector.tensor_copy(xn[:, blk(b)], y_bank[b]).then_inc(out_copied_dve, 1)

        @block.tensor
        def _(pe):
            def mm3(out, w_hi_ap, w_lo_ap, x_hi_ap, x_lo_ap, start, stop, skip=False):
                nc.tensor.matmul(out, w_hi_ap, x_hi_ap, start=start, stop=False, skip_group_check=skip)
                nc.tensor.matmul(out, w_hi_ap, x_lo_ap, start=False, stop=False, skip_group_check=skip)
                return nc.tensor.matmul(out, w_lo_ap, x_hi_ap, start=False, stop=stop, skip_group_check=skip)

            def layer_norm(turn):
                for b in range(NB):
                    if turn == 0:
                        pe.wait_ge(x_landed[b], 16)
                    nc.tensor.matmul(mean_bank[b], ones_mean[:], res[:, blk(b)], start=True, stop=True
                                     ).then_inc(ln_mean, 1)
                for b in range(NB):
                    pe.wait_ge(ln_sq, turn * NB + b + 1)
                    for t in range(4):
                        mm = nc.tensor.matmul(y_bank[b][:, t:t + 1], sq[:, tile(4 * b + t)], ones_mean[:, 0:1],
                                              start=True, stop=True)
                    mm.then_inc(ln_var, 1)
                for b in range(NB):
                    pe.wait_ge(ln_rstd, turn * NB + b + 1)
                    for t in range(4 * b, 4 * b + 4):
                        mm = nc.tensor.matmul(mean_bank[b][:, tile(t % 4)], rstd[:, t:t + 1].broadcast_to([P, P]),
                                              ident[:], start=True, stop=True)
                    mm.then_inc(ln_spread, 1)

            def background_task(task, k, bank, h, s, pair):
                wait(pe, bg_drained, k - BGRING + 1)
                if task[0] == "qk":
                    b = task[1]
                    if b == 0:
                        pe.wait_ge(w_lo_ready, h + 1)
                    mm3(bg[:, bank], w_hi[s][:], w_lo[s][:], xn_hi[:, blk(b)], xn_lo[:, blk(b)], True, True
                        ).then_inc(bg_ready, 1)
                elif task[0] == "v":
                    for r in range(4):
                        mm = nc.tensor.matmul(bg[:, bank, tile(r)], xn[:, tile(4 * task[1] + r)],
                                              w_raw[s][:, D:3 * D], start=True, stop=True)
                    mm.then_inc(bg_ready, 1)
                elif task[0] == "max":
                    t, c = task[1:]
                    if t % 4 == 0 and c == 0:
                        pe.wait_ge(q_dup_landed[t // 4], h * 16 + 16)
                        pe.wait_ge(k_lo_ready, h * NB + t // 4 + 1)
                    width = max_width(t, c)
                    wide = max(256, width)
                    diagonal = c == t // 4
                    mm = nc.tensor.matmul(bg[:, bank, 0:wide], q_hihi[s][:, tile(t)],
                                          k_lohi[s][:, c * BLK:c * BLK + wide], start=True, stop=not diagonal)
                    if diagonal:
                        mm = nc.tensor.matmul(bg[:, bank, width - P:width], ident_bf[:], mask_rows[:],
                                              start=False, stop=True)
                    mm.then_inc(bg_ready, 1)
                elif task[0] == "shift":
                    pe.wait_ge(neg_max_ready, h + 1)
                    nc.tensor.transpose(bg[0:NT, bank, 0:P], neg_max[:], ident[:]).then_inc(bg_ready, 1)
                elif task[0] == "att_t":
                    b = task[1]
                    pe.wait_ge(attn_ready, (pair * 2 + 1) * NB + b + 1)
                    for r in range(4):
                        mm = nc.tensor.transpose(bg[:, bank, tile(r)], attn[:, 4 * b + r, :], ident[:])
                    mm.then_inc(bg_ready, 1)
                elif task[0] == "att_y":
                    pe.wait_ge(wo_lo_ready, pair + 1)
                    pe.wait_ge(att_lo_ready, pair * NB + task[1] + 1)
                    mm3(bg[:, bank], wo_hi[:], wo_lo[:], att_hi[:], att_lo[:], True, True).then_inc(bg_ready, 1)

            def scores(h, s, n, k):
                G = h * NG + n
                b, p = GROUPS[n]
                lo, hi = columns(n)
                if k == 0:
                    wait(pe, exp_done, G - STRING + 1)
                if k == 0 and n == 0:
                    pe.wait_ge(shift_landed, h * 16 + 16)
                    pe.wait_ge(q_lo_ready, h * NB + NB)
                    pe.wait_ge(k_dup_landed, h * 16 + 16)
                kt = 2 * p + k
                out = st[:, n % STRING, k, lo:hi]
                q = slice(b * BLK + lo, b * BLK + hi)
                diagonal = kt >= 4 * b
                nc.tensor.matmul(out, k_lohi[s][:, tile(kt)], q_hihi[s][:, q], start=True, stop=False)
                mm = nc.tensor.matmul(out, k_hi_one[s][0:D + 1, tile(kt)], q_lo_shift[s][0:D + 1, q],
                                      start=False, stop=not diagonal)
                if diagonal:
                    j = kt - 4 * b
                    mm = nc.tensor.matmul(st[:, n % STRING, k, tile(j)], ident_bf[:], mask_cols[:],
                                          start=False, stop=True)
                if k == 1:
                    mm.then_inc(st_ready, 1)

            def p_times_v(h, s, n, k):
                b, p = GROUPS[n]
                if k == 0:
                    if n == 0:
                        pe.wait_ge(v_lo_ready, h * 4 + 4)
                    if p == 0:
                        wait(pe, pv_drained, h * NB + b)
                    pe.wait_ge(*lo_sem(h, n))
                kt = 2 * p + k
                for j in range(max(0, kt - 4 * b), 4):
                    out = pv4[:, j // 2, j % 2, :]
                    cols = slice(k * BLK + j * P, k * BLK + (j + 1) * P)
                    nc.tensor.matmul(out, p_hi[:, n % PRING, cols], v_parts[s][:, kt, :],
                                     start=(kt == 0 and j % 2 == 0), stop=False, skip_group_check=True)
                    mm = nc.tensor.matmul(out[:, 0:D + 1], p_lo[:, n % PRING, cols], v_parts[s][:, kt, 0:D + 1],
                                          start=False, stop=(kt == 4 * b + j), skip_group_check=True)
                if k == 1:
                    mm.then_inc(p_used, 1)

            pe.wait_ge(ones_ready, 2)
            layer_norm(0)
            pe.wait_ge(xn_lo_ready, NB)
            pe.wait_ge(consts, N_CONST)
            for k, task in enumerate(PROLOGUE):
                background_task(task, k, bg_bank(k), 0, 0, None)

            def body(i, first, last):
                base, at = bg_base(i, first), bg_base(0 if first else 1, first)
                for s in range(2):
                    h = i * 2 + s
                    slots = background(s, first, last)
                    for n in range(NG):
                        m = (n - LAG) % NG
                        units = [(scores, h, s, n, 0), (scores, h, s, n, 1)]
                        if m < n:
                            units += [(p_times_v, h, s, m, 0), (p_times_v, h, s, m, 1)]
                        elif not (first and s == 0):
                            units += [(p_times_v, h - 1, 1 - s, m, 0), (p_times_v, h - 1, 1 - s, m, 1)]
                        for item in spread(units, slots[n]):
                            if callable(item[0]):
                                item[0](*item[1:])
                                continue
                            background_task(item, base, bg_bank(at), h + 1, 1 - s, i if s else i - 1)
                            base, at = base + 1, at + 1

            pe.wait_ge(one_rows, 2)
            pairs(pe, body)
            for n in range(NG - LAG, NG):
                for k in range(2):
                    p_times_v(H - 1, 1, n, k)
            for k, task in zip((BG_TOTAL - 2, BG_TOTAL - 1), TAIL):
                background_task(task, k, bg_bank(k), None, None, PAIRS - 1)
            pe.wait_ge(bg_drained, BG_TOTAL)
            layer_norm(1)

            pe.wait_ge(xn_ready, 2 * NB)
            for t in range(NT):
                mm = nc.tensor.matmul(st[:, 0, 0, t * EXPERTS:(t + 1) * EXPERTS], xn[:, tile(t)], gate_w[:],
                                      start=True, stop=True)
            mm.then_inc(logits_ready, 1)
            pe.wait_ge(comb_ready, 1)
            for t in range(NT):
                mm = nc.tensor.transpose(mean_bank[t // 4][0:EXPERTS, tile(t % 4)], comb[:, t, :], ident[:])
            mm.then_inc(comb_t_ready, 1)

            for b in range(NB):
                nc.tensor.matmul(y_bank[b], ident[:], res[:, blk(b)], start=True, stop=False, skip_group_check=True)
            pe.wait_ge(xn_lo_ready, 2 * NB)
            pe.wait_ge(comb_t_copied, NB)

            def down(Q, s, q, final):
                b, c = divmod(q, FC)
                d = slice((2 * FC + c) * P, (2 * FC + c + 1) * P)
                pe.wait_ge(h_lo_ready, Q + 1)
                mm3(y_bank[b], e_hi[s][:, d], e_lo[s][:, d], h_hi[q % HRING], h_lo[:, q % HRING],
                    False, final and c == FC - 1, skip=True).then_inc(down_done, 1)

            def body(p, s, first, last):
                pe.wait_ge(e_lo_ready, p + 1)
                for q in range(STEPS):
                    Q = p * STEPS + q
                    b, c = divmod(q, FC)
                    wait(pe, h_ready, Q - 1)
                    g = slice(c * P, (c + 1) * P)
                    u = slice((FC + c) * P, (FC + c + 1) * P)
                    if not first and c == 0:
                        pe.wait_ge(xw_lo_ready, (p - 1) * NB + b + 1)
                    up_hi, up_lo = (xn_hi, xn_lo) if first else (xw_hi[s], xw_lo[s])
                    mm3(st[:, q % 2, 0, :], e_hi[s][:, g], e_lo[s][:, g], xn_hi[:, blk(b)], xn_lo[:, blk(b)],
                        True, True)
                    mm3(st[:, q % 2, 1, :], e_hi[s][:, u], e_lo[s][:, u], up_hi[:, blk(b)], up_lo[:, blk(b)],
                        True, True).then_inc(gu_ready, 1)
                    m = (q - FLAG) % STEPS
                    if m < q:
                        down(Q - FLAG, s, m, last)
                    elif not first:
                        down(Q - FLAG, 1 - s, m, False)

            passes(pe, body)
            for q in range(STEPS - FLAG, STEPS):
                down(8 * STEPS + q, 1, q, True)


def kernel(L0_attn_x, L0_attn_qkv_w, L0_attn_qkv_b, L0_attn_out_w, L0_attn_out_b, L0_ffn_gate_w,
           L0_ffn_expert_gate, L0_ffn_expert_up, L0_ffn_expert_down, L0_ffn_shared_gate, L0_ffn_shared_up,
           L0_ffn_shared_down):
    import numpy as np
    import concourse.bacc as bacc
    from concourse.bass_utils import run_bass_kernel_spmd

    def rows(*parts):
        return np.concatenate([np.asarray(p) for p in parts], axis=0)

    gates = rows(L0_ffn_expert_gate, np.asarray(L0_ffn_shared_gate)[None])
    ups = rows(L0_ffn_expert_up, np.asarray(L0_ffn_shared_up)[None])
    downs = rows(L0_ffn_expert_down, np.asarray(L0_ffn_shared_down)[None])
    ffn_w = np.zeros((EXPERTS + 1, P, 3 * FC * P), np.float32)
    ffn_w[:, :, 0:F] = gates.transpose(0, 2, 1)
    ffn_w[:, :, FC * P:FC * P + F] = ups.transpose(0, 2, 1)
    down_t = np.zeros((EXPERTS + 1, FC * P, P), np.float32)
    down_t[:, 0:F, :] = downs.transpose(0, 2, 1)
    ffn_w[:, :, 2 * FC * P:] = down_t.reshape(EXPERTS + 1, FC, P, P).transpose(0, 2, 1, 3).reshape(
        EXPERTS + 1, P, FC * P)
    bias = np.asarray(L0_attn_qkv_b)
    arrays = {
        "x_t": np.asarray(L0_attn_x)[0].T,
        "qkv_w": np.asarray(L0_attn_qkv_w),
        "qk_bias_in": bias[:, 0:2 * D].reshape(H, P, 1),
        "v_bias": bias[:, 2 * D:3 * D],
        "out_w": np.asarray(L0_attn_out_w).reshape(H * D, P),
        "out_bias": np.asarray(L0_attn_out_b).reshape(P, 1),
        "gate_w_t": np.asarray(L0_ffn_gate_w).T,
        "ffn_w": ffn_w,
    }
    arrays = {n: np.ascontiguousarray(a) for n, a in arrays.items()}
    nc = bacc.Bacc("TRN2", target_bir_lowering=False, num_devices=1)
    args = [nc.dram_tensor(n, a.shape, mybir.dt.from_np(a.dtype), kind="ExternalInput").ap()
            for n, a in arrays.items()]
    args.append(nc.dram_tensor("out_t", (P, T), F32, kind="ExternalOutput").ap())
    layer_kernel(nc, *args)
    r = run_bass_kernel_spmd(nc, [arrays], core_ids=[0])
    return np.ascontiguousarray(np.asarray(r.results[0]["out_t"]).T)[None]
```
